# Optimizing a Trainium2 kernel written in Bass

```python
import numpy as np
import jax
import jax.numpy as jnp

def _softmax(x, axis=-1):
    return jax.nn.softmax(x, axis=axis)

def _gelu(x):
    return jax.nn.gelu(x, approximate=True)

def _silu(x):
    return jax.nn.silu(x)

def _sigmoid(x):
    return jax.nn.sigmoid(x)

def _layernorm(x, axis=-1, eps=1e-05):
    m = jnp.mean(x, axis=axis, keepdims=True)
    v = jnp.var(x, axis=axis, keepdims=True)
    return (x - m) / jnp.sqrt(v + eps)

def _scatter_add(tgt, idx, src, axis=0):
    return tgt.at[idx].add(src)

def _segment_sum(src, seg, n):
    return jax.ops.segment_sum(src, seg, n)
kernel_name = 'mk_adj_ffn_d1_adj_r2_ae4b2f'

def setup_inputs(seed: int=0):
    np.random.seed(seed)
    _w = jnp.asarray

    def _rec_inputs():
        import jax
        import jax.numpy as jnp
        _gk = jax.random.key(seed)
        x = -0.0005207 + 1.001 * jax.random.normal(jax.random.fold_in(_gk, 1), (8, 1024, 128), jnp.float32)
        _a = jax.random.bernoulli(jax.random.fold_in(_gk, 2), 0.00390625, (1024, 1024))
        _a = jnp.logical_or(_a, jnp.swapaxes(_a, -1, -2))
        _a = jnp.logical_or(_a, jnp.eye(1024, dtype=bool))
        adj = _a.astype(jnp.int32)
        return (x, adj)
    x, adj = _rec_inputs()

    def _L0_gnn_setup():
        import jax, jax.numpy as jnp
        import numpy as np
        import math
        CHUNK = 128
        NUM_HEADS = 4
        EPS = 1e-05
        key = jax.random.key(seed)
        ks = jax.random.split(key, 12)
        B, N, F = (4, 1024, 128)
        x = jax.random.normal(ks[0], (B, N, F), dtype=jnp.float32)
        adj_matrix = jax.random.randint(ks[1], (N, N), 0, 2, dtype=jnp.int32)
        s = 1.0 / math.sqrt(F)
        Wq = jax.random.normal(ks[2], (F, F), dtype=jnp.float32) * s
        bq = jnp.zeros((F,), dtype=jnp.float32)
        Wk = jax.random.normal(ks[3], (F, F), dtype=jnp.float32) * s
        bk = jnp.zeros((F,), dtype=jnp.float32)
        Wv = jax.random.normal(ks[4], (F, F), dtype=jnp.float32) * s
        bv = jnp.zeros((F,), dtype=jnp.float32)
        Wo = jax.random.normal(ks[5], (F, F), dtype=jnp.float32) * s
        bo = jnp.zeros((F,), dtype=jnp.float32)
        gamma = jnp.ones((F,), dtype=jnp.float32)
        beta = jnp.zeros((F,), dtype=jnp.float32)
        return {'x': x, 'adj_matrix': adj_matrix, 'Wq': Wq, 'bq': bq, 'Wk': Wk, 'bk': bk, 'Wv': Wv, 'bv': bv, 'Wo': Wo, 'bo': bo, 'gamma': gamma, 'beta': beta}
    _L0_gnn_all = _L0_gnn_setup()
    _L0_gnn_in = {k: v for k, v in _L0_gnn_all.items() if k in ('Wq', 'bq', 'Wk', 'bk', 'Wv', 'bv', 'Wo', 'bo', 'gamma', 'beta')}
    del _L0_gnn_all

    def _L0_ffn_setup():
        import jax, jax.numpy as jnp
        import numpy as np
        D_MODEL = 128
        EXPERT_DIM = 256
        NUM_EXPERTS = 8
        TOP_K = 2
        SEQ_LEN = 1024
        BATCH = 2
        key = jax.random.key(seed)
        ks = jax.random.split(key, 8)
        s = 0.02
        x = jax.random.normal(ks[0], (SEQ_LEN, BATCH, D_MODEL), dtype=jnp.float32)
        Wg = jax.random.normal(ks[1], (D_MODEL, NUM_EXPERTS), dtype=jnp.float32) * s
        bg = jax.random.normal(ks[2], (NUM_EXPERTS,), dtype=jnp.float32) * s
        bias = jnp.zeros((NUM_EXPERTS,), dtype=jnp.float32)
        W1 = jax.random.normal(ks[3], (NUM_EXPERTS, D_MODEL, EXPERT_DIM), dtype=jnp.float32) * s
        b1 = jax.random.normal(ks[4], (NUM_EXPERTS, EXPERT_DIM), dtype=jnp.float32) * s
        W2 = jax.random.normal(ks[5], (NUM_EXPERTS, EXPERT_DIM, D_MODEL), dtype=jnp.float32) * s
        b2 = jax.random.normal(ks[6], (NUM_EXPERTS, D_MODEL), dtype=jnp.float32) * s
        return {'x': x, 'Wg': Wg, 'bg': bg, 'bias': bias, 'W1': W1, 'b1': b1, 'W2': W2, 'b2': b2}
    _L0_ffn_all = _L0_ffn_setup()
    _L0_ffn_in = {k: v for k, v in _L0_ffn_all.items() if k in ('Wg', 'bg', 'bias', 'W1', 'b1', 'W2', 'b2')}
    del _L0_ffn_all
    return {'x': x, 'adj': adj, 'L0_gnn_Wq': _L0_gnn_in['Wq'], 'L0_gnn_bq': _L0_gnn_in['bq'], 'L0_gnn_Wk': _L0_gnn_in['Wk'], 'L0_gnn_bk': _L0_gnn_in['bk'], 'L0_gnn_Wv': _L0_gnn_in['Wv'], 'L0_gnn_bv': _L0_gnn_in['bv'], 'L0_gnn_Wo': _L0_gnn_in['Wo'], 'L0_gnn_bo': _L0_gnn_in['bo'], 'L0_gnn_gamma': _L0_gnn_in['gamma'], 'L0_gnn_beta': _L0_gnn_in['beta'], 'L0_ffn_Wg': _L0_ffn_in['Wg'], 'L0_ffn_bg': _L0_ffn_in['bg'], 'L0_ffn_bias': _L0_ffn_in['bias'], 'L0_ffn_W1': _L0_ffn_in['W1'], 'L0_ffn_b1': _L0_ffn_in['b1'], 'L0_ffn_W2': _L0_ffn_in['W2'], 'L0_ffn_b2': _L0_ffn_in['b2']}

def reference(x, adj, L0_gnn_Wq, L0_gnn_bq, L0_gnn_Wk, L0_gnn_bk, L0_gnn_Wv, L0_gnn_bv, L0_gnn_Wo, L0_gnn_bo, L0_gnn_gamma, L0_gnn_beta, L0_ffn_Wg, L0_ffn_bg, L0_ffn_bias, L0_ffn_W1, L0_ffn_b1, L0_ffn_W2, L0_ffn_b2):
    import jax
    import jax.numpy as jnp

    def _L0_gnn_ref(x, adj_matrix, Wq, bq, Wk, bk, Wv, bv, Wo, bo, gamma, beta):
        import jax, jax.numpy as jnp
        import numpy as np
        import math
        CHUNK = 128
        NUM_HEADS = 4
        EPS = 1e-05
        B, N, Fin = x.shape
        H = NUM_HEADS
        Dout = Wq.shape[0]
        Dh = Dout // H
        Nc = N // CHUNK
        q = (x @ Wq.T + bq).reshape(B, N, H, Dh).transpose(0, 2, 1, 3)
        k = (x @ Wk.T + bk).reshape(B, N, H, Dh).transpose(0, 2, 1, 3)
        v = (x @ Wv.T + bv).reshape(B, N, H, Dh).transpose(0, 2, 1, 3)
        kc = k.reshape(B, H, Nc, CHUNK, Dh)
        vc = v.reshape(B, H, Nc, CHUNK, Dh)
        scores = jnp.einsum('bhnd,bhjcd->bhnjc', q, kc) / jnp.sqrt(jnp.asarray(Dh, dtype=q.dtype))
        scores = jnp.clip(scores, -10.0, 10.0)
        mask = adj_matrix.reshape(N, Nc, CHUNK)[None, None]
        scores = jnp.where(mask == 0, jnp.asarray(-10.0, scores.dtype), scores)
        attn = jax.nn.softmax(scores, axis=-1)
        ctx = jnp.einsum('bhnjc,bhjcd->bhnd', attn, vc)
        ctx = ctx.transpose(0, 2, 1, 3).reshape(B, N, Dout)
        out = ctx @ Wo.T + bo
        out = out + x
        mu = jnp.mean(out, axis=-1, keepdims=True)
        var = jnp.mean(jnp.square(out - mu), axis=-1, keepdims=True)
        out = (out - mu) * jax.lax.rsqrt(var + EPS) * gamma + beta
        return out

    def _L0_ffn_ref(x, Wg, bg, bias, W1, b1, W2, b2):
        import jax, jax.numpy as jnp
        import numpy as np
        D_MODEL = 128
        EXPERT_DIM = 256
        NUM_EXPERTS = 8
        TOP_K = 2
        SEQ_LEN = 1024
        BATCH = 2
        x_flat = x.reshape(-1, D_MODEL)
        gate_logits = x_flat @ Wg + bg + bias
        topk_vals, topk_idx = jax.lax.top_k(gate_logits, TOP_K)
        topk_w = jax.nn.softmax(topk_vals, axis=-1)
        combine = (jax.nn.one_hot(topk_idx, NUM_EXPERTS, dtype=x.dtype) * topk_w[..., None]).sum(axis=1)
        h = jax.nn.relu(jnp.einsum('td,edh->teh', x_flat, W1) + b1)
        y = jnp.einsum('teh,ehd->ted', h, W2) + b2
        out = jnp.einsum('ted,te->td', y, combine)
        return out.reshape(x.shape)
    x = x + _L0_gnn_ref(_layernorm(x, axis=-1), adj, L0_gnn_Wq, L0_gnn_bq, L0_gnn_Wk, L0_gnn_bk, L0_gnn_Wv, L0_gnn_bv, L0_gnn_Wo, L0_gnn_bo, L0_gnn_gamma, L0_gnn_beta)
    x = x + _L0_ffn_ref(_layernorm(x, axis=-1), L0_ffn_Wg, L0_ffn_bg, L0_ffn_bias, L0_ffn_W1, L0_ffn_b1, L0_ffn_W2, L0_ffn_b2)
    return x

_drawn_inputs = setup_inputs


def setup_inputs(seed=0):
    import zlib

    import numpy as np

    out = dict(_drawn_inputs(seed))
    spreads = {'L0_gnn_bq': (0.0, 0.566),
     'L0_gnn_bk': (0.0, 2.0),
     'L0_gnn_bv': (0.0, 0.1),
     'L0_gnn_bo': (0.0, 0.331),
     'L0_gnn_gamma': (1.0, 0.2),
     'L0_gnn_beta': (0.0, 0.1),
     'L0_ffn_bias': (0.0, 0.454)}
    factors = {'L0_ffn_Wg': 2.89,
     'L0_ffn_bg': 8.0,
     'L0_ffn_W1': 3.163,
     'L0_ffn_b1': 29.758,
     'L0_ffn_b2': 6.473}
    for name, (base, spread) in spreads.items():
        noise = np.random.default_rng([zlib.crc32(name.encode()), seed]).standard_normal(out[name].shape)
        drawn = base * np.exp(spread * noise) if base else spread * noise
        out[name] = jnp.asarray(drawn.astype(out[name].dtype))
    for name, factor in factors.items():
        out[name] = (out[name] * factor).astype(out[name].dtype)
    return out
```

```python
from contextlib import ExitStack

import numpy as np

import concourse.bass as bass
from concourse import mybir

F32 = mybir.dt.float32
F32R = mybir.dt.float32r
BF16 = mybir.dt.bfloat16
I32 = mybir.dt.int32
ALU = mybir.AluOpType
ACT = mybir.ActivationFunctionType
AX_X = mybir.AxisListType.X

P = 128
HEADS = 4
DH = P // HEADS
GROUPS = 32
LAG = 3
EPS = 1e-5
E_HI = float(np.exp(np.float32(10.0)))
E_LO = float(np.exp(np.float32(-10.0)))
FAR = 1.0e30
NO_EDGE = -float(2.0 ** 60)
ADDED = (0, 2, 4, 6)
BOUNDED = (1, 3, 5, 7)
STEPS = 19


def at_least(eng, sem, value):
    if isinstance(value, int) and value <= 0:
        return
    eng.wait_ge(sem, value)


def gnn_moe_kernel(nc, x, adjT, WqT, WkT, WvT, WoT, bq, bk, bv, bo, gamma, beta,
                   Wg, bg, bias, W1, b1, W2, b2, out):
    B, N, F = x.shape[0], adjT.shape[0], WqT.shape[0]
    KT = N // P
    HALF = N // 2
    E = Wg.shape[1]
    HID = W1.shape[1] // E
    NH = HID // P
    SCALE = float(1.0 / np.sqrt(np.float32(DH)))

    ctx = ExitStack()
    with ctx:
        def sb(name, shape, dt=F32):
            return ctx.enter_context(nc.sbuf_tensor(name, shape, dt))

        def ps(name, shape, dt=F32):
            return ctx.enter_context(nc.psum_tensor(name, shape, dt))

        def sem(name):
            return ctx.enter_context(nc.semaphore(name))

        xn_dram = nc.dram_tensor("xn_scratch", [B, P, KT * F], F32, kind="Internal").ap()
        x1_dram = nc.dram_tensor("x1_scratch", [B, P, KT * F], F32, kind="Internal").ap()
        x3T_dram = nc.dram_tensor("x3T_scratch", [B, P, N], F32, kind="Internal").ap()
        c_dram = nc.dram_tensor("c_scratch", [B, P, KT * E], F32, kind="Internal").ap()
        den_dram = nc.dram_tensor("den_scratch", [HEADS, KT, HALF], F32, kind="Internal").ap()
        rden_dram = nc.dram_tensor("rden_scratch", [HEADS, KT, HALF], F32, kind="Internal").ap()

        score_ps = ps("score_ps", [P, 3, HALF])
        ctx_ps = ps("ctx_ps", [P, 2, HALF])
        den_ps = ps("den_ps", [P, HALF])
        pre_ps = ps("pre_ps", [P, 512])
        post_ps = ps("post_ps", [P, 512])

        addmask = sb("addmask", [P, len(ADDED), N], BF16)
        clipmask = sb("clipmask", [P, len(BOUNDED), N])
        kstack = sb("kstack", [P, HEADS, N], F32R)
        qstack = sb("qstack", [P, HEADS, N], F32R)
        vfull = sb("vfull", [P, KT, F])
        exps = sb("exps", [P, 2, 2, HALF])
        probs = sb("probs", [P, 4, 2, HALF])
        ctxu = sb("ctxu", [P, 2 * KT, HALF])
        rdenB = sb("rdenB", [P, KT, HALF])
        den = sb("den", [P, HALF])
        den_sq, rden_sq = sb("den_sq", [P, P]), sb("rden_sq", [P, P])
        xpre = sb("xpre", [P, KT, F])
        xn = sb("xn", [P, KT, F])
        xnT = sb("xnT", [P, N])
        q_hi, q_lo = sb("q_hi", [P, N], F32R), sb("q_lo", [P, N], F32R)
        k_hi, k_lo = sb("k_hi", [P, N], F32R), sb("k_lo", [P, N], F32R)
        vnew = sb("vnew", [P, KT, F])
        ctxn = sb("ctxn", [P, N])
        xnpost, xpost = sb("xnpost", [P, KT, F]), sb("xpost", [P, KT, F])
        attn = sb("attn", [P, KT, F])
        x1 = sb("x1", [P, KT, F])
        x3 = sb("x3", [P, KT, F])
        x3T = sb("x3T", [P, N])
        wq, wk, wv, wo = (sb(f"w{n}_sb", [P, F]) for n in "qkvo")
        bq_c, bk_c = sb("bq_c", [P, 1]), sb("bk_c", [P, 1])
        bv_b, bo_b, gamma_b, beta_b = (sb(f"{n}_b", [P, F]) for n in ("bv", "bo", "gamma", "beta"))
        wg_sb = sb("wg_sb", [P, E])
        bg_b, bias_b, gateb = sb("bg_b", [P, E]), sb("bias_b", [P, E]), sb("gateb", [P, E])
        ident = sb("ident", [P, P])
        ident16 = sb("ident16", [P, P], BF16)
        onehot = sb("onehot", [P, KT, DH])
        eps8, mhalf8 = sb("eps8", [P, KT]), sb("mhalf8", [P, KT])
        rank = sb("rank", [P, E])
        st = [sb(f"st{n}", [P, KT, 6]) for n in range(3)]
        mean2, mdif, vsum, mdif2, var = ([sb(f"{v}{n}", [P, KT]) for n in range(3)]
                                         for v in ("mean2_", "mdif_", "vsum_", "mdif2_", "var_"))
        veps = [sb(f"veps{n}", [P, KT]) for n in range(3)]
        rstd = [sb(f"rstd{n}", [P, KT]) for n in range(3)]
        nm = [sb(f"nm{n}", [P, KT]) for n in range(3)]
        shift = [sb(f"shift{n}", [P, KT]) for n in range(3)]
        lg, lg2, eq, cand = (sb(n, [P, KT, E]) for n in ("lg", "lg2", "eq", "cand"))
        oh1, oh2, cmb1, cmb2, comb = (sb(n, [P, KT, E]) for n in ("oh1", "oh2", "cmb1", "cmb2", "comb"))
        m1, m2, r1, r2, dm, ed, es, w1st, w2nd = (sb(n, [P, KT]) for n in
                                                  ("m1", "m2", "r1", "r2", "dm", "ed", "es", "w1st", "w2nd"))
        b1_c = sb("b1_c", [P, E * NH])
        cch = sb("cch", [P, 2, 4 * E])

        adj_sb = ctxu[:].rearrange("p (t a) n -> p t (a n)", a=2)
        slots = E * HID // HALF
        w1_sb = ctxu[:, 0:slots, :].rearrange("p s n -> p (s n)")
        w2_sb = ctxu[:, slots:2 * slots, :].rearrange("p s n -> p (s n)")
        b2_b = ctxu[:, 2 * slots:2 * slots + E * F // HALF, :].rearrange("p s n -> p (s n)")
        hidden = exps
        xch = [probs[:, s, 0, :] for s in range(2)]
        acc = [probs[:, s, 1, :] for s in range(2)]

        consts_in = sem("consts_in")
        wproj_in = sem("wproj_in")
        adj_in = sem("adj_in")
        fills = sem("fills")
        fill_dve = sem("fill_dve")
        xpre_in = sem("xpre_in")
        stats = [sem(f"stats{n}") for n in range(3)]
        norm_ready = [sem(f"norm_ready{n}") for n in range(3)]
        xn_done = sem("xn_done")
        xn_stored = sem("xn_stored")
        pre_mm = sem("pre_mm")
        pre_act = sem("pre_act")
        pre_dve = sem("pre_dve")
        q_in = [sem(f"q_in{c}") for c in range(2)]
        k_in = [sem(f"k_in{c}") for c in range(2)]
        v_in = [sem(f"v_in{c}") for c in range(2)]
        qk_done = sem("qk_done")
        exp_done = sem("exp_done")
        clip_done = sem("clip_done")
        pv_done = sem("pv_done")
        ctx_out = sem("ctx_out")
        den_out = sem("den_out")
        den_stored = sem("den_stored")
        den_in = sem("den_in")
        rden_done = sem("rden_done")
        rden_stored = sem("rden_stored")
        rdenB_in = sem("rdenB_in")
        product_done = sem("product_done")
        sum_done = sem("sum_done")
        post_in = sem("post_in")
        xpost_in = sem("xpost_in")
        xnb_done = sem("xnb_done")
        xpb_done = sem("xpb_done")
        o_mm = sem("o_mm")
        o_done = sem("o_done")
        ln2_done = sem("ln2_done")
        x1_done = sem("x1_done")
        x1_stored = sem("x1_stored")
        x3_done = sem("x3_done")
        g_mm = sem("g_mm")
        x3T_done = sem("x3T_done")
        x3T_stored = sem("x3T_stored")
        top_dve = sem("top_dve")
        ed_done = sem("ed_done")
        c_stored = sem("c_stored")

        moe_w = sem("moe_w")
        chunk_in = [sem(f"chunk_in{n}") for n in range(2)]
        hid_mm = sem("hid_mm")
        hid_done = sem("hid_done")
        y_mm = sem("y_mm")
        acc_y = sem("acc_y")
        acc_b = sem("acc_b")
        out_stored = [sem(f"out_stored{n}") for n in range(2)]

        block = ctx.enter_context(nc.Block())

        def iterations(eng, body, last=B - 2):
            def step(i):
                body(i, att=i < B, pre=i + 1 < B, first=1 <= i <= B, second=2 <= i <= B + 1, third=i >= 3)

            for i in range(3):
                step(i)
            with eng.Fori(3, last + 1) as i:
                body(i, att=True, pre=True, first=True, second=True, third=True)
            for i in range(last + 1, B + 3):
                step(i)

        @block.sync
        def _(sp):
            def load_xpre(j):
                at_least(sp, xn_done, KT * j)
                sp.dma_start(xpre[:].rearrange("p t f -> p (t f)"),
                             x[bass.ds(j, 1)].rearrange("a p n -> p (a n)")).then_inc(xpre_in, 16)

            def hand_q(j, half):
                sp.wait_ge(pre_dve, 6 * j + 3 + 2 * half)
                cols = slice(half * HALF, (half + 1) * HALF)
                for h in range(HEADS):
                    for r in range(4):
                        sp.dma_start(qstack[DH * r:DH * r + DH, h, cols].bitcast(F32),
                                     (q_hi, q_lo)[r % 2][DH * h:DH * h + DH, cols].bitcast(F32)).then_inc(q_in[half], 16)

            def hand_k(j, half):
                sp.wait_ge(pre_dve, 6 * j + 4 + 2 * half)
                cols = slice(half * HALF, (half + 1) * HALF)
                for h in range(HEADS):
                    for r in range(4):
                        sp.dma_start(kstack[DH * r:DH * r + DH, h, cols].bitcast(F32),
                                     (k_hi, k_lo)[r // 2][DH * h:DH * h + DH, cols].bitcast(F32)).then_inc(k_in[half], 16)

            def hand_v(j, half):
                at_least(sp, pv_done, GROUPS * (j - 1) + 24 + 8 * half)
                sp.dma_start(vfull[:, 4 * half:4 * half + 4, :], vnew[:, 4 * half:4 * half + 4, :]).then_inc(v_in[half], 16)

            def store_xn(j):
                sp.wait_ge(xn_done, KT * j + KT)
                sp.dma_start(xn_dram[bass.ds(j, 1)].rearrange("a p n -> p (a n)"),
                             xn[:].rearrange("p t f -> p (t f)")).then_inc(xn_stored, 16)

            sp.dma_start(xpre[:].rearrange("p t f -> p (t f)"),
                         x[0:1].rearrange("a p n -> p (a n)")).then_inc(xpre_in, 16)
            for w, src in ((wq, WqT), (wk, WkT), (wv, WvT)):
                sp.dma_start(w[:], src).then_inc(wproj_in, 16)
            for c, src in ((bq_c, bq), (bk_c, bk)):
                sp.dma_start(c[:], src.rearrange("(p a) -> p a", a=1)).then_inc(wproj_in, 16)
            for t in range(KT):
                sp.dma_start(adj_sb[:, t, :].bitcast(I32), adjT[t * P:(t + 1) * P, :]).then_inc(adj_in, 16)

            store_xn(0)
            load_xpre(1)
            hand_q(0, 0)
            hand_k(0, 0)
            hand_v(0, 0)

            def body(i, att, pre, first, second, third):
                if att:
                    hand_v(i, 1)
                    hand_k(i, 1)
                    hand_q(i, 1)
                if first:
                    if second:
                        sp.wait_ge(o_done, 2 * (i - 2) + 2)
                    sp.wait_ge(xn_stored, 16 * (i - 1) + 16)
                    sp.dma_start(xnpost[:].rearrange("p t f -> p (t f)"),
                                 xn_dram[bass.ds(i - 1, 1)].rearrange("a p n -> p (a n)")).then_inc(post_in, 16)
                if pre:
                    store_xn(i + 1)
                    if not isinstance(i, int) or i + 2 < B:
                        load_xpre(i + 2)
                if third:
                    sp.wait_ge(top_dve, STEPS * (i - 3) + STEPS)
                    sp.dma_start(c_dram[bass.ds(i - 3, 1)].rearrange("a p n -> p (a n)"),
                                 comb[:].rearrange("p t e -> p (t e)")).then_inc(c_stored, 16)
                if second:
                    sp.wait_ge(x1_done, 2 * (i - 2) + 2)
                    sp.dma_start(x1_dram[bass.ds(i - 2, 1)].rearrange("a p n -> p (a n)"),
                                 x1[:].rearrange("p t f -> p (t f)")).then_inc(x1_stored, 16)
                if first:
                    sp.dma_start(xpost[:].rearrange("p t f -> p (t f)"),
                                 x[bass.ds(i - 1, 1)].rearrange("a p n -> p (a n)")).then_inc(xpost_in, 16)
                if pre:
                    hand_q(i + 1, 0)
                    hand_k(i + 1, 0)
                    hand_v(i + 1, 0)
                if second:
                    sp.wait_ge(x3T_done, 2 * (i - 2) + 2)
                    sp.dma_start(x3T_dram[bass.ds(i - 2, 1)].rearrange("a p n -> p (a n)"), x3T[:]).then_inc(x3T_stored, 16)

            iterations(sp, body, last=B - 3)

            sp.wait_ge(x1_stored, 16 * B)
            sp.wait_ge(x3T_stored, 16 * B)
            sp.wait_ge(c_stored, 16 * B)
            sp.wait_ge(pv_done, GROUPS * B)

            def load_chunk(k, s):
                sp.dma_start(xch[s], x3T_dram[bass.ds(k, 1), :, s * 512:(s + 1) * 512].rearrange("a p n -> p (a n)")
                             ).then_inc(chunk_in[s], 16)
                sp.dma_start(acc[s], x1_dram[bass.ds(k, 1), :, s * 512:(s + 1) * 512].rearrange("a p n -> p (a n)")
                             ).then_inc(chunk_in[s], 16)
                sp.dma_start(cch[:, s], c_dram[bass.ds(k, 1), :, s * 32:(s + 1) * 32].rearrange("a p n -> p (a n)")
                             ).then_inc(chunk_in[s], 16)

            def store_chunk(k, s):
                sp.wait_ge(acc_b, E * (2 * k + s) + E)
                sp.dma_start(out[bass.ds(k, 1), :, s * 512:(s + 1) * 512].rearrange("a p n -> p (a n)"), acc[s]
                             ).then_inc(out_stored[s], 16)

            load_chunk(0, 0)
            load_chunk(0, 1)
            with sp.Fori(0, B - 1) as k:
                for s in range(2):
                    store_chunk(k, s)
                    sp.wait_ge(out_stored[s], 16 * k + 16)
                    load_chunk(k + 1, s)
            for s in range(2):
                store_chunk(B - 1, s)
            for s in range(2):
                sp.wait_ge(out_stored[s], 16 * B)

        @block.tensor
        def _(pe):
            def scores(i, g):
                half, kt, pair = g // 16, g % 16 // 2, g % 2
                cols = slice(half * HALF, (half + 1) * HALF)
                if g in (0, 16):
                    pe.wait_ge(q_in[half], 256 * (i + 1))
                if g in (0, 8):
                    pe.wait_ge(k_in[g // 8], 256 * (i + 1))
                for hh in range(2):
                    tile = 2 * g + hh
                    at_least(pe, exp_done, 64 * i + max(tile - 2, 0))
                    mm = pe.matmul(score_ps[:, tile % 3, :], kstack[:, 2 * pair + hh, kt * P:(kt + 1) * P],
                                   qstack[:, 2 * pair + hh, cols], start=True, stop=kt in BOUNDED)
                    if kt in ADDED:
                        mm = pe.matmul(score_ps[:, tile % 3, :], ident16[:], addmask[:, ADDED.index(kt), cols],
                                       start=False, stop=True)
                    mm.then_inc(qk_done, 1)

            def context(i, g):
                half, kt, pair = g // 16, g % 16 // 2, g % 2
                if g in (0, 8):
                    pe.wait_ge(v_in[g // 8], 16 * (i + 1))
                pe.wait_ge(clip_done, GROUPS * i + g + 1)
                if pair == 0:
                    at_least(pe, ctx_out, 16 * i + 8 * half + kt - 1)
                for hh in range(2):
                    c = 64 * pair + DH * hh
                    pe.matmul(ctx_ps[c:c + DH, kt % 2, :], vfull[:, kt, c:c + DH],
                              probs[:, g % 4, hh, :], start=True, stop=True)
                if g % 16 == 0:
                    at_least(pe, den_out, 2 * i + half)
                for hh in range(2):
                    c = 64 * (1 - pair) + DH * hh
                    mm = pe.matmul(den_ps[c:c + DH, :], onehot[:, kt, :], probs[:, g % 4, hh, :],
                                   start=(kt == 0), stop=(kt == KT - 1))
                mm.then_inc(pv_done, 1)

            def prepare(j, u):
                if u == 0:
                    at_least(pe, pre_dve, 6 * j)
                elif u <= 2:
                    pe.wait_ge(pre_act, 6 * j + u)
                else:
                    pe.wait_ge(pre_dve, 6 * j + u - 2)
                if u < 2:
                    pe.wait_ge(xn_done, KT * j + 4 * u + 4)
                    for t in range(4):
                        mm = pe.transpose(pre_ps[:, t * P:(t + 1) * P], xn[:, 4 * u + t, :], ident[:])
                elif u < 4:
                    for t in range(4):
                        tile = 4 * (u - 2) + t
                        mm = pe.matmul(pre_ps[:, t * P:(t + 1) * P], xnT[:, tile * P:(tile + 1) * P], wv[:],
                                       start=True, stop=True)
                else:
                    half = u // 2 - 2
                    mm = pe.matmul(pre_ps[:], (wq, wk)[u % 2][:], xnT[:, half * HALF:(half + 1) * HALF],
                                   start=True, stop=True)
                mm.then_inc(pre_mm, 1)

            def project(j, half):
                pe.wait_ge(sum_done, 3 * (2 * j + half) + 3)
                if half == 0:
                    at_least(pe, o_done, 2 * j)
                elif isinstance(j, int) and j == 0:
                    pe.wait_ge(o_done, 1)
                else:
                    pe.wait_ge(top_dve, STEPS * (j - 1) + 1)
                for t in range(4):
                    tile = 4 * half + t
                    mm = pe.matmul(post_ps[:, t * P:(t + 1) * P], ctxn[:, tile * P:(tile + 1) * P], wo[:],
                                   start=True, stop=True)
                mm.then_inc(o_mm, 1)

            def turn_x3(j, half, projected):
                pe.wait_ge(x3_done, KT * j + 4 * half + 4)
                if half == 0:
                    pe.wait_ge(o_done, 2 * (j + 1) + (1 if projected else 0))
                else:
                    pe.wait_ge(x3T_done, 2 * j + 1)
                for t in range(4):
                    mm = pe.transpose(post_ps[:, t * P:(t + 1) * P], x3[:, 4 * half + t, :], ident[:])
                mm.then_inc(g_mm, 1)

            def logits(j):
                pe.wait_ge(x3T_done, 2 * j + 2)
                for t in range(KT):
                    mm = pe.matmul(post_ps[:, t * E:(t + 1) * E], x3T[:, t * P:(t + 1) * P], wg_sb[:],
                                   start=True, stop=True)
                mm.then_inc(g_mm, 1)

            pe.wait_ge(fills, 8 + KT)
            pe.wait_ge(wproj_in, 16 * 5)
            for u in range(8):
                prepare(0, u)
            pe.wait_ge(fill_dve, KT + len(BOUNDED) + 1)

            def body(i, att, pre, first, second, third):
                for g in range(GROUPS):
                    if att:
                        scores(i, g)
                    if g >= LAG and att:
                        context(i, g - LAG)
                    if g < LAG and first:
                        context(i - 1, GROUPS + g - LAG)
                    if pre and g in (7, 9, 11, 14, 17, 22, 25, 28):
                        prepare(i + 1, (7, 9, 11, 14, 17, 22, 25, 28).index(g))
                    if g == 2 and second:
                        project(i - 2, 1)
                    if g == 18 and first:
                        if isinstance(i, int) and i == 1:
                            pe.wait_ge(consts_in, 16 * 8)
                        project(i - 1, 0)
                    if second:
                        if g in (25, 27):
                            turn_x3(i - 2, (g - 25) // 2, first)
                        if g == 29:
                            logits(i - 2)

            iterations(pe, body)

            def hidden_units(k, s, e):
                H = E * (2 * k + s) + e
                if e == 0:
                    pe.wait_ge(chunk_in[s], 48 * k + 48)
                for h in range(NH):
                    at_least(pe, hid_done, NH * (H - 1) + h + 1)
                    pe.matmul(score_ps[:, h, :], w1_sb[:, (e * NH + h) * P:(e * NH + h + 1) * P], xch[s],
                              start=True, stop=True).then_inc(hid_mm, 1)

            def expert_output(k, s, e):
                H = E * (2 * k + s) + e
                pe.wait_ge(hid_done, NH * (H + 1))
                at_least(pe, acc_y, H - 1)
                for t in range(4):
                    for h in range(NH):
                        mm = pe.matmul(ctx_ps[:, e % 2, t * P:(t + 1) * P],
                                       hidden[:, e % 2, h, t * P:(t + 1) * P],
                                       w2_sb[:, (e * NH + h) * F:(e * NH + h + 1) * F],
                                       start=(h == 0), stop=(h == NH - 1))
                mm.then_inc(y_mm, 1)

            pe.wait_ge(moe_w, 16 * 4)
            pe.wait_ge(exp_done, 64 * B)
            pe.wait_ge(ctx_out, 16 * B)

            def chunk(k, s, first):
                for e in range(E):
                    hidden_units(k, s, e)
                    if e > 0:
                        expert_output(k, s, e - 1)
                    elif not first:
                        expert_output(k if s else k - 1, 1 - s, E - 1)

            chunk(0, 0, True)
            chunk(0, 1, False)
            with pe.Fori(1, B) as k:
                for s in range(2):
                    chunk(k, s, False)
            expert_output(B - 1, 1, E - 1)

        @block.scalar
        def _(act):
            def exponentials(i, g):
                G = GROUPS * i + g
                for hh in range(2):
                    act.wait_ge(qk_done, 2 * G + hh + 1)
                    if hh == 0:
                        at_least(act, clip_done, G - 1)
                    act.activation(exps[:, g % 2, hh, :], score_ps[:, (2 * g + hh) % 3, :], ACT.Exp,
                                   scale=SCALE).then_inc(exp_done, 1)

            def copy_context(i, half, kt):
                act.wait_ge(pv_done, GROUPS * i + 16 * half + 2 * kt + 2)
                if kt % 2 == 0:
                    at_least(act, product_done, 8 * (i - 1) + 4 * half + kt // 2 + 1)
                act.activation(ctxu[:, KT * half + kt, :], ctx_ps[:, kt % 2, :], ACT.Copy).then_inc(ctx_out, 1)

            def copy_sums(i, half):
                U = 2 * i + half
                act.wait_ge(pv_done, 16 * (U + 1))
                at_least(act, den_stored, 64 * U)
                act.activation(den[:], den_ps[:], ACT.Copy).then_inc(den_out, 1)

            def store_sums(i, half):
                U = 2 * i + half
                act.wait_ge(den_out, U + 1)
                at_least(act, den_in, 16 * U)
                for h in range(HEADS):
                    row = 64 * (1 - h // 2) + DH * (h % 2)
                    act.dma_start(den_dram[h], den[row:row + KT, :]).then_inc(den_stored, 16)

            def load_sums(i, half):
                U = 2 * i + half
                act.wait_ge(den_stored, 64 * (U + 1))
                at_least(act, rden_done, U)
                act.dma_start(den_sq[:], den_dram.rearrange("h j (a n) -> (h j a) n", n=P)).then_inc(den_in, 16)

            def store_reciprocals(i, half):
                U = 2 * i + half
                act.wait_ge(rden_done, U + 1)
                at_least(act, rdenB_in, 16 * U)
                act.dma_start(rden_dram.rearrange("h j (a n) -> (h j a) n", n=P), rden_sq[:]).then_inc(rden_stored, 16)

            def spread_reciprocals(i, half):
                U = 2 * i + half
                act.wait_ge(rden_stored, 16 * (U + 1))
                at_least(act, sum_done, 3 * U)
                act.dma_start(rdenB[:].rearrange("p j n -> p (j n)"),
                              rden_dram.rearrange("h j n -> h (j n)").unsqueeze(1).to_broadcast([HEADS, DH, KT * HALF])
                              ).then_inc(rdenB_in, 16)

            def normalise(n, j, src, dst, done, tiles):
                for t in tiles:
                    act.activation(dst[:, t, :], src[:, t, :], ACT.Identity, bias=shift[n][:, t:t + 1],
                                   scale=rstd[n][:, t:t + 1]).then_inc(done, 1)

            def first_norm(j, tiles):
                act.wait_ge(norm_ready[0], 4 * j + 4)
                at_least(act, pre_mm, 8 * (j - 1) + 2)
                at_least(act, xn_stored, 16 * j)
                normalise(0, j, xpre, xn, xn_done, tiles)

            def evacuate(j, u):
                act.wait_ge(pre_mm, 8 * j + u + 1)
                if u < 2:
                    act.activation(xnT[:, u * 512:(u + 1) * 512], pre_ps[:], ACT.Copy).then_inc(pre_act, 1)
                else:
                    half = u // 2 - 2
                    at_least(act, (q_in, k_in)[u % 2][half], 256 * j)
                    act.activation((q_hi, k_hi)[u % 2][:, half * HALF:(half + 1) * HALF], pre_ps[:], ACT.Identity,
                                   bias=(bq_c, bk_c)[u % 2][:, 0:1]).then_inc(pre_act, 1)

            act.dma_start(wo[:], WoT).then_inc(consts_in, 16)
            act.dma_start(wg_sb[:], Wg).then_inc(consts_in, 16)
            for t, src in ((bv_b, bv), (bo_b, bo), (gamma_b, gamma), (beta_b, beta), (bg_b, bg), (bias_b, bias)):
                act.dma_start(t[:], src.rearrange("(a f) -> a f", a=1).to_broadcast([P, src.shape[0]])
                              ).then_inc(consts_in, 16)

            act.wait_ge(wproj_in, 16 * 5)
            first_norm(0, range(KT))
            for u in (0, 1, 4, 5, 6, 7):
                evacuate(0, u)
            act.wait_ge(fill_dve, KT + len(BOUNDED) + 1)

            def body(i, att, pre, first, second, third):
                for g in range(GROUPS):
                    if att:
                        exponentials(i, g)
                        if g % 2 and 5 <= g <= 19:
                            copy_context(i, 0, (g - 5) // 2)
                        if g % 2 and g >= 21:
                            copy_context(i, 1, (g - 21) // 2)
                        if g == 18:
                            copy_sums(i, 0)
                        if g == 19:
                            store_sums(i, 0)
                        if g == 21:
                            load_sums(i, 0)
                        if g == 25:
                            store_reciprocals(i, 0)
                        if g == 28:
                            spread_reciprocals(i, 0)
                    if first:
                        if g in (1, 3):
                            copy_context(i - 1, 1, 6 + g // 2)
                        if g == 2:
                            copy_sums(i - 1, 1)
                        if g == 3:
                            store_sums(i - 1, 1)
                        if g == 5:
                            load_sums(i - 1, 1)
                        if g == 9:
                            store_reciprocals(i - 1, 1)
                        if g == 12:
                            spread_reciprocals(i - 1, 1)
                    if pre:
                        if g in (3, 4, 5, 6):
                            first_norm(i + 1, (2 * g - 6, 2 * g - 5))
                        if g in (8, 10, 18, 23, 26, 29):
                            evacuate(i + 1, {8: 0, 10: 1, 18: 4, 23: 5, 26: 6, 29: 7}[g])
                    if second:
                        if g in (9, 10):
                            act.wait_ge(norm_ready[1], 4 * (i - 2) + 4)
                            normalise(1, i - 2, attn, attn, ln2_done, range(4 * (g - 9), 4 * (g - 8)))
                        if g in (23, 24):
                            act.wait_ge(norm_ready[2], 4 * (i - 2) + 4)
                            at_least(act, g_mm, 3 * (i - 2))
                            normalise(2, i - 2, x1, x3, x3_done, range(4 * (g - 23), 4 * (g - 22)))
                        if g in (26, 28):
                            half = (g - 26) // 2
                            if half == 0:
                                at_least(act, x3T_stored, 16 * (i - 2))
                                at_least(act, g_mm, 3 * (i - 2))
                            act.wait_ge(g_mm, 3 * (i - 2) + half + 1)
                            act.activation(x3T[:, half * 512:(half + 1) * 512], post_ps[:], ACT.Copy
                                           ).then_inc(x3T_done, 1)
                    if third and g == 14:
                        act.wait_ge(top_dve, STEPS * (i - 3) + 12)
                        act.activation(ed[:], dm[:], ACT.Exp).then_inc(ed_done, 1)

            iterations(act, body)

            act.wait_ge(product_done, 8 * B)
            act.dma_start(w1_sb, W1).then_inc(moe_w, 16)
            act.dma_start(w2_sb, W2).then_inc(moe_w, 16)
            act.dma_start(b1_c[:], b1).then_inc(moe_w, 16)
            act.dma_start(b2_b, b2.rearrange("(a e) f -> a (e f)", a=1).to_broadcast([P, E * F])).then_inc(moe_w, 16)
            act.wait_ge(clip_done, GROUPS * B)
            act.wait_ge(moe_w, 16 * 4)

            def relus(k, s):
                for e in range(E):
                    H = E * (2 * k + s) + e
                    at_least(act, y_mm, H - 1)
                    for h in range(NH):
                        act.wait_ge(hid_mm, NH * H + h + 1)
                        act.activation(hidden[:, e % 2, h, :], score_ps[:, h, :], ACT.Relu,
                                       bias=b1_c[:, e * NH + h:e * NH + h + 1]).then_inc(hid_done, 1)

            for s in range(2):
                relus(0, s)
            with act.Fori(1, B) as k:
                for s in range(2):
                    relus(k, s)

        @block.vector
        def _(dve):
            def clip(i, g):
                half, kt = g // 16, g % 16 // 2
                G = GROUPS * i + g
                dve.wait_ge(exp_done, 2 * G + 2)
                at_least(dve, pv_done, G - 3)
                if kt in ADDED:
                    dve.tensor_scalar(probs[:, g % 4], exps[:, g % 2], E_LO, E_HI, ALU.max, ALU.min
                                      ).then_inc(clip_done, 1)
                else:
                    m = BOUNDED.index(kt)
                    dve.scalar_tensor_tensor(probs[:, g % 4], exps[:, g % 2], E_LO,
                                             clipmask[:, m:m + 1, half * HALF:(half + 1) * HALF].to_broadcast([P, 2, HALF]),
                                             ALU.max, ALU.min).then_inc(clip_done, 1)

            def statistics(n, j, src):
                at_least(dve, norm_ready[n], 4 * j)
                for t in range(KT):
                    ins = dve.bn_stats(st[n][:, t, :], src[:, t, :])
                ins.then_inc(stats[n], 1)
                dve.wait_ge(stats[n], 4 * j + 1)
                s = st[n]
                dve.tensor_tensor(mean2[n][:], s[:, :, 1], s[:, :, 4], ALU.add)
                dve.tensor_tensor(mdif[n][:], s[:, :, 1], s[:, :, 4], ALU.subtract)
                dve.tensor_tensor(vsum[n][:], s[:, :, 2], s[:, :, 5], ALU.add).then_inc(stats[n], 1)
                dve.wait_ge(stats[n], 4 * j + 2)
                dve.scalar_tensor_tensor(mdif2[n][:], mdif[n][:], 0.25, mdif[n][:], ALU.mult, ALU.mult).then_inc(stats[n], 1)
                dve.wait_ge(stats[n], 4 * j + 3)
                dve.scalar_tensor_tensor(var[n][:], vsum[n][:], 1.0 / F, mdif2[n][:], ALU.mult, ALU.add
                                         ).then_inc(stats[n], 1)

            def evacuate(j, u):
                if u < 4:
                    dve.wait_ge(pre_mm, 8 * j + u + 1)
                    at_least(dve, v_in[u - 2], 16 * j)
                    dve.tensor_tensor(vnew[:, 4 * (u - 2):4 * (u - 1), :],
                                      pre_ps[:].rearrange("p (t f) -> p t f", t=4),
                                      bv_b[:].unsqueeze(1).to_broadcast([P, 4, F]), ALU.add).then_inc(pre_dve, 1)
                else:
                    half = u // 2 - 2
                    cols = slice(half * HALF, (half + 1) * HALF)
                    dve.wait_ge(pre_act, 6 * j + u - 1)
                    dve.scalar_tensor_tensor((q_lo, k_lo)[u % 2][:, cols], pre_ps[:], (bq_c, bk_c)[u % 2][:, 0:1],
                                             (q_hi, k_hi)[u % 2][:, cols].bitcast(F32),
                                             ALU.add, ALU.subtract).then_inc(pre_dve, 1)

            def turn_over(j, half):
                U = 2 * j + half
                dve.wait_ge(den_in, 16 * (U + 1))
                at_least(dve, rden_stored, 16 * U)
                dve.reciprocal(rden_sq[:], den_sq[:]).then_inc(rden_done, 1)

            def divide_contexts(j, half, n):
                U = 2 * j + half
                if n == 0:
                    dve.wait_ge(rdenB_in, 16 * (U + 1))
                    dve.wait_ge(ctx_out, 8 * (U + 1))
                kts = slice(2 * n, 2 * n + 2)
                dve.tensor_tensor(rdenB[:, kts, :], ctxu[:, KT * half + 2 * n:KT * half + 2 * n + 2, :],
                                  rdenB[:, kts, :], ALU.mult).then_inc(product_done, 1)

            def residual(j, half):
                dve.wait_ge(o_mm, 2 * j + half + 1)
                dve.wait_ge(xnb_done, j + 1)
                at_least(dve, x1_done, 2 * j)
                dve.tensor_tensor(attn[:, 4 * half:4 * half + 4, :], post_ps[:].rearrange("p (t f) -> p t f", t=4),
                                  xnpost[:, 4 * half:4 * half + 4, :], ALU.add).then_inc(o_done, 1)

            def top_step(j, n):
                lanes = lambda v: v[:].unsqueeze(2).to_broadcast([P, KT, E])
                ranks = rank[:].unsqueeze(1).to_broadcast([P, KT, E])
                if n > 1:
                    dve.wait_ge(top_dve, STEPS * j + n - 1)
                if n == 1:
                    dve.wait_ge(g_mm, 3 * j + 3)
                    ins = dve.tensor_tensor(lg[:], post_ps[:, 0:KT * E].rearrange("p (t e) -> p t e", e=E),
                                            gateb[:].unsqueeze(1).to_broadcast([P, KT, E]), ALU.add)
                elif n == 2:
                    ins = dve.tensor_reduce(m1[:], lg[:], AX_X, ALU.max)
                elif n == 3:
                    ins = dve.tensor_tensor(eq[:], lg[:], lanes(m1), ALU.is_equal)
                elif n == 4:
                    ins = dve.tensor_tensor(cand[:], eq[:], ranks, ALU.mult)
                elif n == 5:
                    ins = dve.tensor_reduce(r1[:], cand[:], AX_X, ALU.max)
                elif n == 6:
                    ins = dve.tensor_tensor(oh1[:], ranks, lanes(r1), ALU.is_equal)
                elif n == 7:
                    ins = dve.scalar_tensor_tensor(lg2[:], oh1[:], -FAR, lg[:], ALU.mult, ALU.add)
                elif n == 8:
                    ins = dve.tensor_reduce(m2[:], lg2[:], AX_X, ALU.max)
                elif n == 9:
                    ins = dve.tensor_tensor(eq[:], lg2[:], lanes(m2), ALU.is_equal)
                elif n == 10:
                    ins = dve.tensor_tensor(cand[:], eq[:], ranks, ALU.mult)
                elif n == 11:
                    ins = dve.tensor_reduce(r2[:], cand[:], AX_X, ALU.max)
                elif n == 12:
                    ins = dve.tensor_tensor(dm[:], m2[:], m1[:], ALU.subtract)
                elif n == 13:
                    ins = dve.tensor_tensor(oh2[:], ranks, lanes(r2), ALU.is_equal)
                elif n == 14:
                    dve.wait_ge(ed_done, j + 1)
                    ins = dve.tensor_scalar(es[:], ed[:], 1.0, None, ALU.add)
                elif n == 15:
                    ins = dve.reciprocal(w1st[:], es[:])
                elif n == 16:
                    ins = dve.tensor_tensor(w2nd[:], ed[:], w1st[:], ALU.mult)
                elif n == 17:
                    ins = dve.tensor_tensor(cmb1[:], oh1[:], lanes(w1st), ALU.mult)
                elif n == 18:
                    ins = dve.tensor_tensor(cmb2[:], oh2[:], lanes(w2nd), ALU.mult)
                else:
                    at_least(dve, c_stored, 16 * j)
                    ins = dve.tensor_tensor(comb[:], cmb1[:], cmb2[:], ALU.add)
                ins.then_inc(top_dve, 1)

            dve.wait_ge(xpre_in, 16)

            dve.wait_ge(xpre_in, 16)
            statistics(0, 0, xpre)
            for t in range(KT):
                dve.wait_ge(adj_in, 16 * KT)
                if t in ADDED:
                    dve.tensor_scalar(addmask[:, ADDED.index(t), :], adj_sb[:, t, :].bitcast(I32), 0.0, NO_EDGE,
                                      ALU.is_equal, ALU.mult).then_inc(fill_dve, 1)
                else:
                    dve.tensor_scalar(clipmask[:, BOUNDED.index(t), :], adj_sb[:, t, :].bitcast(I32), 0.0, E_HI,
                                      ALU.not_equal, ALU.mult).then_inc(fill_dve, 1)
            dve.wait_ge(fill_dve, KT)
            for m in range(len(BOUNDED)):
                dve.tensor_scalar(clipmask[:, m, :], clipmask[:, m, :], E_LO, None, ALU.max).then_inc(fill_dve, 1)
            dve.wait_ge(wproj_in, 16 * 5)
            dve.wait_ge(consts_in, 16 * 8)
            dve.tensor_tensor(gateb[:], bg_b[:], bias_b[:], ALU.add).then_inc(fill_dve, 1)
            for u in range(2, 8):
                evacuate(0, u)
            dve.wait_ge(fill_dve, KT + len(BOUNDED) + 1)

            def body(i, att, pre, first, second, third):
                for g in range(GROUPS):
                    if att:
                        clip(i, g)
                        if g == 23:
                            turn_over(i, 0)
                    if first:
                        if g in (0, 2, 4, 6):
                            divide_contexts(i - 1, 0, g // 2)
                        if g == 7:
                            turn_over(i - 1, 1)
                        if g in (16, 18, 20, 22):
                            divide_contexts(i - 1, 1, g // 2 - 8)
                        if g == 20:
                            residual(i - 1, 0)
                    if third:
                        if g <= 12:
                            top_step(i - 3, g + 1)
                        if 15 <= g <= 20:
                            top_step(i - 3, g - 1)
                    if second:
                        if g == 4:
                            residual(i - 2, 1)
                        if g == 5:
                            dve.wait_ge(o_done, 2 * (i - 2) + 2)
                            statistics(1, i - 2, attn)
                        if g == 21:
                            dve.wait_ge(x1_done, 2 * (i - 2) + 2)
                            statistics(2, i - 2, x1)
                    if pre:
                        if g == 0:
                            dve.wait_ge(xpre_in, 16 * (i + 1) + 16)
                            statistics(0, i + 1, xpre)
                        if g in (12, 15, 19, 24, 27, 30):
                            evacuate(i + 1, {12: 2, 15: 3, 19: 4, 24: 5, 27: 6, 30: 7}[g])

            iterations(dve, body)

            def combine(k, s):
                dve.wait_ge(chunk_in[s], 48 * k + 48)
                for e in range(E):
                    H = E * (2 * k + s) + e
                    dve.wait_ge(y_mm, H + 1)
                    if e:
                        dve.wait_ge(acc_b, H)
                    for t in range(4):
                        ins = dve.scalar_tensor_tensor(acc[s][:, t * F:(t + 1) * F], ctx_ps[:, e % 2, t * F:(t + 1) * F],
                                                       cch[:, s, t * E + e:t * E + e + 1],
                                                       acc[s][:, t * F:(t + 1) * F], ALU.mult, ALU.add)
                    ins.then_inc(acc_y, 1)
                    dve.wait_ge(acc_y, H + 1)
                    for t in range(4):
                        ins = dve.scalar_tensor_tensor(acc[s][:, t * F:(t + 1) * F], b2_b[:, e * F:(e + 1) * F],
                                                       cch[:, s, t * E + e:t * E + e + 1],
                                                       acc[s][:, t * F:(t + 1) * F], ALU.mult, ALU.add)
                    ins.then_inc(acc_b, 1)

            dve.wait_ge(moe_w, 16 * 4)
            with dve.Fori(0, B) as k:
                for s in range(2):
                    combine(k, s)

        @block.gpsimd
        def _(pool):
            pool.memset(ident[:], 0.0).then_inc(fills, 1)
            pool.memset(onehot[:], 0.0).then_inc(fills, 1)
            pool.memset(eps8[:], EPS).then_inc(fills, 1)
            pool.memset(mhalf8[:], -0.5).then_inc(fills, 1)
            pool.iota(rank[:], pattern=[[-1, E]], base=E, channel_multiplier=0,
                      allow_small_or_imprecise_dtypes=True).then_inc(fills, 1)
            pool.wait_ge(fills, 5)
            pool.affine_select(out=ident[:], in_=ident[:], compare_op=ALU.not_equal, fill=1.0, base=0,
                               pattern=[[-1, P]], channel_multiplier=1).then_inc(fills, 2)
            for t in range(KT):
                pool.memset(onehot[:, t, t:t + 1], 1.0).then_inc(fills, 1)
            pool.wait_ge(fills, 7 + KT)
            pool.tensor_copy(ident16[:], ident[:]).then_inc(fills, 1)

            def scale_and_shift(n, j, used):
                pool.wait_ge(stats[n], 4 * j + 4)
                at_least(pool, used, KT * j)
                pool.tensor_tensor(veps[n][:], var[n][:], eps8[:], ALU.add).then_inc(norm_ready[n], 1)
                pool.wait_ge(norm_ready[n], 4 * j + 1)
                pool.tensor_tensor(rstd[n][:], veps[n][:], mhalf8[:], ALU.pow).then_inc(norm_ready[n], 1)
                pool.wait_ge(norm_ready[n], 4 * j + 2)
                pool.tensor_tensor(nm[n][:], mean2[n][:], rstd[n][:], ALU.mult).then_inc(norm_ready[n], 1)
                pool.wait_ge(norm_ready[n], 4 * j + 3)
                pool.tensor_tensor(shift[n][:], nm[n][:], mhalf8[:], ALU.mult).then_inc(norm_ready[n], 1)

            pool.wait_ge(fills, 8 + KT)
            scale_and_shift(0, 0, xn_done)
            pool.wait_ge(consts_in, 16 * 8)

            def sum_key_tiles(j, half):
                U = 2 * j + half
                pool.wait_ge(product_done, 4 * (U + 1))
                pool.tensor_tensor(rdenB[:, 0:4, :], rdenB[:, 0:4, :], rdenB[:, 4:8, :], ALU.add).then_inc(sum_done, 1)
                pool.wait_ge(sum_done, 3 * U + 1)
                pool.tensor_tensor(rdenB[:, 0:2, :], rdenB[:, 0:2, :], rdenB[:, 2:4, :], ALU.add).then_inc(sum_done, 1)
                pool.wait_ge(sum_done, 3 * U + 2)
                at_least(pool, o_mm, 2 * (j - 1) + half + 1)
                pool.tensor_tensor(ctxn[:, half * HALF:(half + 1) * HALF], rdenB[:, 0, :], rdenB[:, 1, :], ALU.add
                                   ).then_inc(sum_done, 1)

            def body(i, att, pre, first, second, third):
                wide = lambda v: v[:].unsqueeze(1).to_broadcast([P, KT, F])
                if pre:
                    scale_and_shift(0, i + 1, xn_done)
                if second:
                    scale_and_shift(1, i - 2, ln2_done)
                if first:
                    sum_key_tiles(i - 1, 0)
                    pool.wait_ge(post_in, 16 * (i - 1) + 16)
                    pool.tensor_tensor(xnpost[:], xnpost[:], wide(bo_b), ALU.add).then_inc(xnb_done, 1)
                if second:
                    pool.wait_ge(ln2_done, KT * (i - 2) + KT)
                    pool.tensor_tensor(attn[:], attn[:], wide(gamma_b), ALU.mult).then_inc(x1_done, 1)
                    pool.wait_ge(x1_done, 2 * (i - 2) + 1)
                    pool.wait_ge(xpb_done, (i - 2) + 1)
                    at_least(pool, x3_done, KT * (i - 2))
                    at_least(pool, x1_stored, 16 * (i - 2))
                    pool.tensor_tensor(x1[:], attn[:], xpost[:], ALU.add).then_inc(x1_done, 1)
                    scale_and_shift(2, i - 2, x3_done)
                if first:
                    pool.wait_ge(xpost_in, 16 * (i - 1) + 16)
                    pool.tensor_tensor(xpost[:], xpost[:], wide(beta_b), ALU.add).then_inc(xpb_done, 1)
                    sum_key_tiles(i - 1, 1)

            iterations(pool, body)



_INS = ["x", "adjT", "WqT", "WkT", "WvT", "WoT", "bq", "bk", "bv", "bo", "gamma", "beta",
        "Wg", "bg", "bias", "W1", "b1", "W2", "b2"]


def kernel(x, adj, L0_gnn_Wq, L0_gnn_bq, L0_gnn_Wk, L0_gnn_bk, L0_gnn_Wv, L0_gnn_bv, L0_gnn_Wo, L0_gnn_bo,
           L0_gnn_gamma, L0_gnn_beta, L0_ffn_Wg, L0_ffn_bg, L0_ffn_bias, L0_ffn_W1, L0_ffn_b1, L0_ffn_W2, L0_ffn_b2):
    import concourse.bacc as bacc
    from concourse.bass_utils import run_bass_kernel_spmd

    B, N, F = x.shape
    E, _, HID = L0_ffn_W1.shape
    KT, NH = N // P, HID // P
    flat = lambda a: np.ascontiguousarray(np.asarray(a))
    laid = {
        "x": flat(np.asarray(x).reshape(B, KT, P, F).transpose(0, 2, 1, 3).reshape(B, P, KT * F)),
        "adjT": flat(np.asarray(adj).T),
        "WqT": flat(np.asarray(L0_gnn_Wq).T), "WkT": flat(np.asarray(L0_gnn_Wk).T),
        "WvT": flat(np.asarray(L0_gnn_Wv).T), "WoT": flat(np.asarray(L0_gnn_Wo).T),
        "bq": flat(L0_gnn_bq), "bk": flat(L0_gnn_bk), "bv": flat(L0_gnn_bv), "bo": flat(L0_gnn_bo),
        "gamma": flat(L0_gnn_gamma), "beta": flat(L0_gnn_beta),
        "Wg": flat(L0_ffn_Wg), "bg": flat(L0_ffn_bg), "bias": flat(L0_ffn_bias),
        "W1": flat(np.asarray(L0_ffn_W1).transpose(1, 0, 2).reshape(F, E * HID)),
        "b1": flat(np.asarray(L0_ffn_b1).reshape(E * NH, P).T),
        "W2": flat(np.asarray(L0_ffn_W2).reshape(E * NH, P, F).transpose(1, 0, 2).reshape(P, E * NH * F)),
        "b2": flat(L0_ffn_b2),
    }
    nc = bacc.Bacc("TRN2", target_bir_lowering=False, num_devices=1)
    args = [nc.dram_tensor(f"in_{n}", laid[n].shape, mybir.dt.from_np(laid[n].dtype), kind="ExternalInput").ap()
            for n in _INS]
    out = nc.dram_tensor("out_0", (B, P, KT * F), F32, kind="ExternalOutput").ap()
    gnn_moe_kernel(nc, *args, out)
    got = run_bass_kernel_spmd(nc, [{f"in_{n}": laid[n] for n in _INS}], core_ids=[0]).results[0]["out_0"]
    return np.ascontiguousarray(got.reshape(B, P, KT, F).transpose(0, 2, 1, 3).reshape(B, N, F))
```

```python
from contextlib import ExitStack

import numpy as np

import concourse.bass as bass
from concourse import mybir

F32 = mybir.dt.float32
F32R = mybir.dt.float32r
BF16 = mybir.dt.bfloat16
I32 = mybir.dt.int32
ALU = mybir.AluOpType
ACT = mybir.ActivationFunctionType
AX_X = mybir.AxisListType.X

P = 128
HEADS = 4
DH = P // HEADS
GROUPS = 32
LAG = 3
EPS = 1e-5
E_HI = float(np.exp(np.float32(10.0)))
E_LO = float(np.exp(np.float32(-10.0)))
FAR = 1.0e30
NO_EDGE = -float(2.0 ** 60)
ADDED = (0, 2, 4, 6)
BOUNDED = (1, 3, 5, 7)
STEPS = 19


def at_least(eng, sem, value):
    if isinstance(value, int) and value <= 0:
        return
    eng.wait_ge(sem, value)


def gnn_moe_kernel(nc, x, adjT, WqT, WkT, WvT, WoT, bq, bk, bv, bo, gamma, beta,
                   Wg, bg, bias, W1, b1, W2, b2, out):
    B, N, F = x.shape[0], adjT.shape[0], WqT.shape[0]
    KT = N // P
    HALF = N // 2
    E = Wg.shape[1]
    HID = W1.shape[1] // E
    NH = HID // P
    SCALE = float(1.0 / np.sqrt(np.float32(DH)))

    ctx = ExitStack()
    with ctx:
        def sb(name, shape, dt=F32):
            return ctx.enter_context(nc.sbuf_tensor(name, shape, dt))

        def ps(name, shape, dt=F32):
            return ctx.enter_context(nc.psum_tensor(name, shape, dt))

        def sem(name):
            return ctx.enter_context(nc.semaphore(name))

        xn_dram = nc.dram_tensor("xn_scratch", [B, P, KT * F], F32, kind="Internal").ap()
        x1_dram = nc.dram_tensor("x1_scratch", [B, P, KT * F], F32, kind="Internal").ap()
        x3T_dram = nc.dram_tensor("x3T_scratch", [B, P, N], F32, kind="Internal").ap()
        c_dram = nc.dram_tensor("c_scratch", [B, P, KT * E], F32, kind="Internal").ap()
        q_dram, k_dram = (nc.dram_tensor(f"{n}_scratch", [4, DH, HEADS, N], F32, kind="Internal").ap() for n in "qk")
        den_dram = nc.dram_tensor("den_scratch", [HEADS, KT, HALF], F32, kind="Internal").ap()
        rden_dram = nc.dram_tensor("rden_scratch", [HEADS, KT, HALF], F32, kind="Internal").ap()

        score_ps = ps("score_ps", [P, 2, 2, HALF])
        ctx_ps = ps("ctx_ps", [P, 2, HALF])
        den_ps = ps("den_ps", [P, HALF])
        side_ps = ps("side_ps", [P, 512])

        addmask = sb("addmask", [P, len(ADDED), N], BF16)
        clipmask = sb("clipmask", [P, len(BOUNDED), N])
        kstack = sb("kstack", [P, HEADS, N], F32R)
        qstack = sb("qstack", [P, HEADS, N], F32R)
        vfull = sb("vfull", [P, KT, F])
        exps = sb("exps", [P, 2, 2, HALF])
        probs = sb("probs", [P, 4, 2, HALF])
        ctxu = sb("ctxu", [P, 2 * KT, HALF])
        rdenB = sb("rdenB", [P, KT, HALF])
        den = sb("den", [P, HALF])
        den_sq, rden_sq = sb("den_sq", [P, P]), sb("rden_sq", [P, P])
        xpre = sb("xpre", [P, KT, F])
        xn = sb("xn", [P, KT, F])
        xnT = sb("xnT", [P, N])
        q_hi, q_lo = sb("q_hi", [P, N], F32R), sb("q_lo", [P, N], F32R)
        k_hi, k_lo = sb("k_hi", [P, N], F32R), sb("k_lo", [P, N], F32R)
        vnew = sb("vnew", [P, KT, F])
        ctxn = sb("ctxn", [P, N])
        xnpost, xpost = sb("xnpost", [P, KT, F]), sb("xpost", [P, KT, F])
        attn = sb("attn", [P, KT, F])
        x1 = sb("x1", [P, KT, F])
        x3 = sb("x3", [P, KT, F])
        x3T = sb("x3T", [P, N])
        wq, wk, wv, wo = (sb(f"w{n}_sb", [P, F]) for n in "qkvo")
        bq_c, bk_c = sb("bq_c", [P, 1]), sb("bk_c", [P, 1])
        bv_b, bo_b, gamma_b, beta_b = (sb(f"{n}_b", [P, F]) for n in ("bv", "bo", "gamma", "beta"))
        wg_sb = sb("wg_sb", [P, E])
        bg_b, bias_b, gateb = sb("bg_b", [P, E]), sb("bias_b", [P, E]), sb("gateb", [P, E])
        ident = sb("ident", [P, P])
        ident16 = sb("ident16", [P, P], BF16)
        onehot = sb("onehot", [P, KT, DH])
        eps8, mhalf8 = sb("eps8", [P, KT]), sb("mhalf8", [P, KT])
        rank = sb("rank", [P, E])
        st = [sb(f"st{n}", [P, KT, 6]) for n in range(3)]
        mean2, mdif, vsum, mdif2, var = ([sb(f"{v}{n}", [P, KT]) for n in range(3)]
                                         for v in ("mean2_", "mdif_", "vsum_", "mdif2_", "var_"))
        veps = [sb(f"veps{n}", [P, KT]) for n in range(3)]
        rstd = [sb(f"rstd{n}", [P, KT]) for n in range(3)]
        nm = [sb(f"nm{n}", [P, KT]) for n in range(3)]
        shift = [sb(f"shift{n}", [P, KT]) for n in range(3)]
        lg, lg2, eq, cand = (sb(n, [P, KT, E]) for n in ("lg", "lg2", "eq", "cand"))
        oh1, oh2, cmb1, cmb2, comb = (sb(n, [P, KT, E]) for n in ("oh1", "oh2", "cmb1", "cmb2", "comb"))
        m1, m2, r1, r2, dm, ed, es, w1st, w2nd = (sb(n, [P, KT]) for n in
                                                  ("m1", "m2", "r1", "r2", "dm", "ed", "es", "w1st", "w2nd"))
        b1_c = sb("b1_c", [P, E * NH])
        cch = sb("cch", [P, 2, 4 * E])

        adj_sb = ctxu[:].rearrange("p (t a) n -> p t (a n)", a=2)
        slots = E * HID // HALF
        w1_sb = ctxu[:, 0:slots, :].rearrange("p s n -> p (s n)")
        w2_sb = ctxu[:, slots:2 * slots, :].rearrange("p s n -> p (s n)")
        b2_b = ctxu[:, 2 * slots:2 * slots + E * F // HALF, :].rearrange("p s n -> p (s n)")
        hidden = exps
        xch = [probs[:, s, 0, :] for s in range(2)]
        acc = [probs[:, s, 1, :] for s in range(2)]

        consts_in = sem("consts_in")
        wproj_in = sem("wproj_in")
        adj_in = sem("adj_in")
        fills = sem("fills")
        fill_dve = sem("fill_dve")
        xpre_in = sem("xpre_in")
        stats = [sem(f"stats{n}") for n in range(3)]
        norm_ready = [sem(f"norm_ready{n}") for n in range(3)]
        xn_done = sem("xn_done")
        xn_stored = sem("xn_stored")
        pre_mm = sem("pre_mm")
        pre_act = sem("pre_act")
        pre_dve = sem("pre_dve")
        q_stored = [sem(f"q_stored{c}") for c in range(2)]
        k_stored = [sem(f"k_stored{c}") for c in range(2)]
        q_in = [sem(f"q_in{c}") for c in range(2)]
        k_in = [sem(f"k_in{c}") for c in range(2)]
        v_in = [sem(f"v_in{c}") for c in range(2)]
        qk_done = sem("qk_done")
        exp_done = sem("exp_done")
        clip_done = sem("clip_done")
        pv_done = sem("pv_done")
        ctx_out = sem("ctx_out")
        den_out = sem("den_out")
        den_stored = sem("den_stored")
        den_in = sem("den_in")
        rden_done = sem("rden_done")
        rden_stored = sem("rden_stored")
        rdenB_in = sem("rdenB_in")
        product_done = sem("product_done")
        sum_done = sem("sum_done")
        post_in = sem("post_in")
        xpost_in = sem("xpost_in")
        xnb_done = sem("xnb_done")
        xpb_done = sem("xpb_done")
        o_mm = sem("o_mm")
        o_done = sem("o_done")
        ln2_done = sem("ln2_done")
        x1_done = sem("x1_done")
        x1_stored = sem("x1_stored")
        x3_done = sem("x3_done")
        g_mm = sem("g_mm")
        x3T_done = sem("x3T_done")
        x3T_stored = sem("x3T_stored")
        top_dve = sem("top_dve")
        ed_done = sem("ed_done")
        c_stored = sem("c_stored")

        moe_w = sem("moe_w")
        chunk_in = [sem(f"chunk_in{n}") for n in range(2)]
        hid_mm = sem("hid_mm")
        hid_done = sem("hid_done")
        y_mm = sem("y_mm")
        acc_y = sem("acc_y")
        acc_b = sem("acc_b")
        out_stored = [sem(f"out_stored{n}") for n in range(2)]

        block = ctx.enter_context(nc.Block())

        def iterations(eng, body, last=B - 2):
            def step(i):
                body(i, att=i < B, pre=i + 1 < B, first=1 <= i <= B, second=2 <= i <= B + 1, third=i >= 3)

            for i in range(4):
                step(i)
            with eng.Fori(4, last + 1) as i:
                body(i, att=True, pre=True, first=True, second=True, third=True)
            for i in range(last + 1, B + 3):
                step(i)

        @block.sync
        def _(sp):
            def load_xpre(j):
                at_least(sp, xn_done, KT * j)
                sp.dma_start(xpre[:].rearrange("p t f -> p (t f)"),
                             x[bass.ds(j, 1)].rearrange("a p n -> p (a n)")).then_inc(xpre_in, 16)

            def store_parts(j, half, n):
                sp.wait_ge(pre_dve, 6 * j + 3 + 2 * n + half)
                cols = slice(half * HALF, (half + 1) * HALF)
                for row, src in enumerate(((q_hi, q_lo, q_hi, q_lo), (k_hi, k_hi, k_lo, k_lo))[n]):
                    sp.dma_start((q_dram, k_dram)[n][row, :, :, cols].rearrange("d h n -> h d n"),
                                 src[:, cols].bitcast(F32)).then_inc((q_stored, k_stored)[n][half], 16)

            def stack_q(j, half):
                sp.wait_ge(q_stored[half], 64 * j + 64)
                cols = slice(half * HALF, (half + 1) * HALF)
                sp.dma_start(qstack[:, :, cols].bitcast(F32),
                             q_dram[:, :, :, cols].rearrange("r d h n -> (r d) h n")).then_inc(q_in[half], 16)

            def stack_k(j, half):
                sp.wait_ge(k_stored[half], 64 * j + 64)
                cols = slice(half * HALF, (half + 1) * HALF)
                sp.dma_start(kstack[:, :, cols].bitcast(F32),
                             k_dram[:, :, :, cols].rearrange("r d h n -> (r d) h n")).then_inc(k_in[half], 16)

            def hand_v(j, half):
                at_least(sp, pv_done, GROUPS * (j - 1) + 24 + 8 * half)
                sp.dma_start(vfull[:, 4 * half:4 * half + 4, :], vnew[:, 4 * half:4 * half + 4, :]).then_inc(v_in[half], 16)

            def store_xn(j):
                sp.wait_ge(xn_done, KT * j + KT)
                sp.dma_start(xn_dram[bass.ds(j, 1)].rearrange("a p n -> p (a n)"),
                             xn[:].rearrange("p t f -> p (t f)")).then_inc(xn_stored, 16)

            sp.dma_start(xpre[:].rearrange("p t f -> p (t f)"),
                         x[0:1].rearrange("a p n -> p (a n)")).then_inc(xpre_in, 16)
            for w, src in ((wq, WqT), (wk, WkT), (wv, WvT)):
                sp.dma_start(w[:], src).then_inc(wproj_in, 16)
            for c, src in ((bq_c, bq), (bk_c, bk)):
                sp.dma_start(c[:], src.rearrange("(p a) -> p a", a=1)).then_inc(wproj_in, 16)
            for t in range(KT):
                sp.dma_start(adj_sb[:, t, :].bitcast(I32), adjT[t * P:(t + 1) * P, :]).then_inc(adj_in, 16)

            store_xn(0)
            load_xpre(1)
            store_parts(0, 0, 0)
            store_parts(0, 1, 0)
            stack_q(0, 0)
            store_parts(0, 0, 1)
            store_parts(0, 1, 1)
            stack_k(0, 0)
            hand_v(0, 0)

            def body(i, att, pre, first, second, third):
                if att:
                    hand_v(i, 1)
                    stack_k(i, 1)
                    stack_q(i, 1)
                if third:
                    sp.wait_ge(x3T_done, 2 * (i - 3) + 2)
                    sp.dma_start(x3T_dram[bass.ds(i - 3, 1)].rearrange("a p n -> p (a n)"), x3T[:]).then_inc(x3T_stored, 16)
                if first:
                    if second:
                        sp.wait_ge(o_done, 2 * (i - 2) + 2)
                    sp.wait_ge(xn_stored, 16 * (i - 1) + 16)
                    sp.dma_start(xnpost[:].rearrange("p t f -> p (t f)"),
                                 xn_dram[bass.ds(i - 1, 1)].rearrange("a p n -> p (a n)")).then_inc(post_in, 16)
                if pre:
                    store_xn(i + 1)
                    if not isinstance(i, int) or i + 2 < B:
                        load_xpre(i + 2)
                    store_parts(i + 1, 0, 0)
                    stack_q(i + 1, 0)
                    store_parts(i + 1, 1, 0)
                if second:
                    sp.wait_ge(x1_done, 2 * (i - 2) + 2)
                    sp.dma_start(x1_dram[bass.ds(i - 2, 1)].rearrange("a p n -> p (a n)"),
                                 x1[:].rearrange("p t f -> p (t f)")).then_inc(x1_stored, 16)
                if first:
                    sp.dma_start(xpost[:].rearrange("p t f -> p (t f)"),
                                 x[bass.ds(i - 1, 1)].rearrange("a p n -> p (a n)")).then_inc(xpost_in, 16)
                if pre:
                    store_parts(i + 1, 0, 1)
                    stack_k(i + 1, 0)
                    hand_v(i + 1, 0)
                if third:
                    sp.wait_ge(top_dve, STEPS * (i - 3) + STEPS)
                    sp.dma_start(c_dram[bass.ds(i - 3, 1)].rearrange("a p n -> p (a n)"),
                                 comb[:].rearrange("p t e -> p (t e)")).then_inc(c_stored, 16)
                if pre:
                    store_parts(i + 1, 1, 1)

            iterations(sp, body, last=B - 3)

            sp.wait_ge(x1_stored, 16 * B)
            sp.wait_ge(x3T_stored, 16 * B)
            sp.wait_ge(c_stored, 16 * B)
            sp.wait_ge(pv_done, GROUPS * B)

            def load_chunk(k, s):
                sp.dma_start(xch[s], x3T_dram[bass.ds(k, 1), :, s * 512:(s + 1) * 512].rearrange("a p n -> p (a n)")
                             ).then_inc(chunk_in[s], 16)
                sp.dma_start(acc[s], x1_dram[bass.ds(k, 1), :, s * 512:(s + 1) * 512].rearrange("a p n -> p (a n)")
                             ).then_inc(chunk_in[s], 16)
                sp.dma_start(cch[:, s], c_dram[bass.ds(k, 1), :, s * 32:(s + 1) * 32].rearrange("a p n -> p (a n)")
                             ).then_inc(chunk_in[s], 16)

            def store_chunk(k, s):
                sp.wait_ge(acc_b, E * (2 * k + s) + E)
                sp.dma_start(out[bass.ds(k, 1), :, s * 512:(s + 1) * 512].rearrange("a p n -> p (a n)"), acc[s]
                             ).then_inc(out_stored[s], 16)

            load_chunk(0, 0)
            load_chunk(0, 1)
            with sp.Fori(0, B - 1) as k:
                for s in range(2):
                    store_chunk(k, s)
                    sp.wait_ge(out_stored[s], 16 * k + 16)
                    load_chunk(k + 1, s)
            for s in range(2):
                store_chunk(B - 1, s)
            for s in range(2):
                sp.wait_ge(out_stored[s], 16 * B)

        @block.tensor
        def _(pe):
            def scores(i, g):
                half, kt, pair = g // 16, g % 16 // 2, g % 2
                cols = slice(half * HALF, (half + 1) * HALF)
                if g in (0, 16):
                    pe.wait_ge(q_in[half], 16 * (i + 1))
                if g in (0, 8):
                    pe.wait_ge(k_in[g // 8], 16 * (i + 1))
                at_least(pe, exp_done, GROUPS * i + g - 1)
                for hh in range(2):
                    mm = pe.matmul(score_ps[:, g % 2, hh, :], kstack[:, 2 * pair + hh, kt * P:(kt + 1) * P],
                                   qstack[:, 2 * pair + hh, cols], start=True, stop=kt in BOUNDED)
                    if kt in ADDED:
                        mm = pe.matmul(score_ps[:, g % 2, hh, :], ident16[:], addmask[:, ADDED.index(kt), cols],
                                       start=False, stop=True)
                mm.then_inc(qk_done, 1)

            def context(i, g):
                half, kt, pair = g // 16, g % 16 // 2, g % 2
                if g in (0, 8):
                    pe.wait_ge(v_in[g // 8], 16 * (i + 1))
                pe.wait_ge(clip_done, GROUPS * i + g + 1)
                if pair == 0:
                    at_least(pe, ctx_out, 16 * i + 8 * half + kt - 1)
                for hh in range(2):
                    c = 64 * pair + DH * hh
                    pe.matmul(ctx_ps[c:c + DH, kt % 2, :], vfull[:, kt, c:c + DH],
                              probs[:, g % 4, hh, :], start=True, stop=True)
                if g % 16 == 0:
                    at_least(pe, den_out, 2 * i + half)
                for hh in range(2):
                    c = 64 * (1 - pair) + DH * hh
                    mm = pe.matmul(den_ps[c:c + DH, :], onehot[:, kt, :], probs[:, g % 4, hh, :],
                                   start=(kt == 0), stop=(kt == KT - 1))
                mm.then_inc(pv_done, 1)

            def prepare(j, u):
                if u < 2:
                    pe.wait_ge(xn_done, KT * j + 4 * u + 4)
                    for t in range(4):
                        mm = pe.transpose(side_ps[:, t * P:(t + 1) * P], xn[:, 4 * u + t, :], ident[:])
                elif u < 4:
                    for t in range(4):
                        tile = 4 * (u - 2) + t
                        mm = pe.matmul(side_ps[:, t * P:(t + 1) * P], xnT[:, tile * P:(tile + 1) * P], wv[:],
                                       start=True, stop=True)
                else:
                    half = u % 2
                    mm = pe.matmul(side_ps[:], (wq, wk)[u // 2 - 2][:], xnT[:, half * HALF:(half + 1) * HALF],
                                   start=True, stop=True)
                mm.then_inc(pre_mm, 1)

            def before_prepare(j, u):
                if u == 0:
                    at_least(pe, pre_dve, 6 * j)
                elif u <= 2:
                    pe.wait_ge(pre_act, 6 * j + u)
                else:
                    pe.wait_ge(pre_dve, 6 * j + u - 2)

            def project(j, half):
                pe.wait_ge(sum_done, 3 * (2 * j + half) + 3)
                for t in range(4):
                    tile = 4 * half + t
                    mm = pe.matmul(side_ps[:, t * P:(t + 1) * P], ctxn[:, tile * P:(tile + 1) * P], wo[:],
                                   start=True, stop=True)
                mm.then_inc(o_mm, 1)

            def turn_x3(j, half):
                pe.wait_ge(x3_done, KT * j + 4 * half + 4)
                for t in range(4):
                    mm = pe.transpose(side_ps[:, t * P:(t + 1) * P], x3[:, 4 * half + t, :], ident[:])
                mm.then_inc(g_mm, 1)

            def logits(j):
                pe.wait_ge(x3T_done, 2 * j + 2)
                for t in range(KT):
                    mm = pe.matmul(side_ps[:, t * E:(t + 1) * E], x3T[:, t * P:(t + 1) * P], wg_sb[:],
                                   start=True, stop=True)
                mm.then_inc(g_mm, 1)

            pe.wait_ge(fills, 8 + KT)
            pe.wait_ge(wproj_in, 16 * 5)
            for u in range(8):
                before_prepare(0, u)
                prepare(0, u)
            pe.wait_ge(fill_dve, KT + len(BOUNDED) + 1)

            def body(i, att, pre, first, second, third):
                for g in range(GROUPS):
                    if att:
                        scores(i, g)
                    if g >= LAG and att:
                        context(i, g - LAG)
                    if g < LAG and first:
                        context(i - 1, GROUPS + g - LAG)
                    if g == 1 and second:
                        if third:
                            pe.wait_ge(x3T_done, 2 * (i - 3) + 2)
                        else:
                            pe.wait_ge(pre_dve, 6 * i + 6)
                        project(i - 2, 1)
                    if g == 3 and third:
                        if second:
                            pe.wait_ge(o_done, 2 * (i - 2) + 2)
                        logits(i - 3)
                    if pre and g in (6, 8, 10, 12, 14, 17):
                        u = (6, 8, 10, 12, 14, 17).index(g)
                        if u > 0:
                            before_prepare(i + 1, u)
                        elif third:
                            pe.wait_ge(top_dve, STEPS * (i - 3) + 1)
                        elif second:
                            pe.wait_ge(o_done, 2 * (i - 2) + 2)
                        else:
                            before_prepare(i + 1, 0)
                        prepare(i + 1, u)
                    if g == 20 and first:
                        if isinstance(i, int) and i == 1:
                            pe.wait_ge(consts_in, 16 * 8)
                        if pre:
                            pe.wait_ge(pre_dve, 6 * (i + 1) + 4)
                        else:
                            pe.wait_ge(top_dve, STEPS * (i - 3) + 1)
                        project(i - 1, 0)
                    if g == 23 and pre:
                        if first:
                            pe.wait_ge(o_done, 2 * (i - 1) + 1)
                        else:
                            before_prepare(i + 1, 6)
                        prepare(i + 1, 6)
                    if g == 26 and second:
                        if pre:
                            pe.wait_ge(pre_dve, 6 * (i + 1) + 5)
                        elif first:
                            pe.wait_ge(o_done, 2 * (i - 1) + 1)
                        else:
                            pe.wait_ge(top_dve, STEPS * (i - 3) + 1)
                        turn_x3(i - 2, 0)
                    if g == 28 and pre:
                        if second:
                            pe.wait_ge(x3T_done, 2 * (i - 2) + 1)
                        else:
                            before_prepare(i + 1, 7)
                        prepare(i + 1, 7)
                    if g == 31 and second:
                        if pre:
                            pe.wait_ge(pre_dve, 6 * (i + 1) + 6)
                        else:
                            pe.wait_ge(x3T_done, 2 * (i - 2) + 1)
                        turn_x3(i - 2, 1)

            iterations(pe, body)

            def hidden_units(k, s, e):
                H = E * (2 * k + s) + e
                if e == 0:
                    pe.wait_ge(chunk_in[s], 48 * k + 48)
                at_least(pe, hid_done, NH * (H - 1))
                for h in range(NH):
                    mm = pe.matmul(score_ps[:, e % 2, h, :], w1_sb[:, (e * NH + h) * P:(e * NH + h + 1) * P], xch[s],
                                   start=True, stop=True)
                mm.then_inc(hid_mm, 1)

            def expert_output(k, s, e):
                H = E * (2 * k + s) + e
                pe.wait_ge(hid_done, NH * (H + 1))
                at_least(pe, acc_y, H - 1)
                for t in range(4):
                    for h in range(NH):
                        mm = pe.matmul(ctx_ps[:, e % 2, t * P:(t + 1) * P],
                                       hidden[:, e % 2, h, t * P:(t + 1) * P],
                                       w2_sb[:, (e * NH + h) * F:(e * NH + h + 1) * F],
                                       start=(h == 0), stop=(h == NH - 1))
                mm.then_inc(y_mm, 1)

            pe.wait_ge(moe_w, 16 * 4)
            pe.wait_ge(exp_done, GROUPS * B)
            pe.wait_ge(ctx_out, 16 * B)

            def chunk(k, s, first):
                for e in range(E):
                    hidden_units(k, s, e)
                    if e > 0:
                        expert_output(k, s, e - 1)
                    elif not first:
                        expert_output(k if s else k - 1, 1 - s, E - 1)

            chunk(0, 0, True)
            chunk(0, 1, False)
            with pe.Fori(1, B) as k:
                for s in range(2):
                    chunk(k, s, False)
            expert_output(B - 1, 1, E - 1)

        @block.scalar
        def _(act):
            def exponentials(i, g):
                G = GROUPS * i + g
                act.wait_ge(qk_done, G + 1)
                at_least(act, clip_done, G - 1)
                act.activation(exps[:, g % 2].rearrange("p h n -> p (h n)"),
                               score_ps[:, g % 2].rearrange("p h n -> p (h n)"), ACT.Exp,
                               scale=SCALE).then_inc(exp_done, 1)

            def copy_context(i, half, kt):
                act.wait_ge(pv_done, GROUPS * i + 16 * half + 2 * kt + 2)
                if kt % 2 == 0:
                    at_least(act, product_done, 8 * (i - 1) + 4 * half + kt // 2 + 1)
                act.activation(ctxu[:, KT * half + kt, :], ctx_ps[:, kt % 2, :], ACT.Copy).then_inc(ctx_out, 1)

            def copy_sums(i, half):
                U = 2 * i + half
                act.wait_ge(pv_done, 16 * (U + 1))
                at_least(act, den_stored, 64 * U)
                act.activation(den[:], den_ps[:], ACT.Copy).then_inc(den_out, 1)

            def store_sums(i, half):
                U = 2 * i + half
                act.wait_ge(den_out, U + 1)
                at_least(act, den_in, 16 * U)
                for h in range(HEADS):
                    row = 64 * (1 - h // 2) + DH * (h % 2)
                    act.dma_start(den_dram[h], den[row:row + KT, :]).then_inc(den_stored, 16)

            def load_sums(i, half):
                U = 2 * i + half
                act.wait_ge(den_stored, 64 * (U + 1))
                at_least(act, rden_done, U)
                act.dma_start(den_sq[:], den_dram.rearrange("h j (a n) -> (h j a) n", n=P)).then_inc(den_in, 16)

            def store_reciprocals(i, half):
                U = 2 * i + half
                act.wait_ge(rden_done, U + 1)
                at_least(act, rdenB_in, 16 * U)
                act.dma_start(rden_dram.rearrange("h j (a n) -> (h j a) n", n=P), rden_sq[:]).then_inc(rden_stored, 16)

            def spread_reciprocals(i, half):
                U = 2 * i + half
                act.wait_ge(rden_stored, 16 * (U + 1))
                at_least(act, sum_done, 3 * U)
                act.dma_start(rdenB[:].rearrange("p j n -> p (j n)"),
                              rden_dram.rearrange("h j n -> h (j n)").unsqueeze(1).to_broadcast([HEADS, DH, KT * HALF])
                              ).then_inc(rdenB_in, 16)

            def normalise(n, j, src, dst, done, tiles):
                for t in tiles:
                    act.activation(dst[:, t, :], src[:, t, :], ACT.Identity, bias=shift[n][:, t:t + 1],
                                   scale=rstd[n][:, t:t + 1]).then_inc(done, 1)

            def first_norm(j, tiles):
                act.wait_ge(norm_ready[0], 4 * j + 4)
                at_least(act, pre_mm, 8 * (j - 1) + 2)
                at_least(act, xn_stored, 16 * j)
                normalise(0, j, xpre, xn, xn_done, tiles)

            def evacuate(j, u):
                act.wait_ge(pre_mm, 8 * j + u + 1)
                if u < 2:
                    act.activation(xnT[:, u * 512:(u + 1) * 512], side_ps[:], ACT.Copy).then_inc(pre_act, 1)
                else:
                    half, n = u % 2, u // 2 - 2
                    at_least(act, (q_in, k_in)[n][half], 16 * j)
                    act.activation((q_hi, k_hi)[n][:, half * HALF:(half + 1) * HALF], side_ps[:], ACT.Identity,
                                   bias=(bq_c, bk_c)[n][:, 0:1]).then_inc(pre_act, 1)

            def copy_turned(j, half):
                act.wait_ge(g_mm, 3 * j + half + 1)
                act.activation(x3T[:, half * 512:(half + 1) * 512], side_ps[:], ACT.Copy).then_inc(x3T_done, 1)

            act.dma_start(wo[:], WoT).then_inc(consts_in, 16)
            act.dma_start(wg_sb[:], Wg).then_inc(consts_in, 16)
            for t, src in ((bv_b, bv), (bo_b, bo), (gamma_b, gamma), (beta_b, beta), (bg_b, bg), (bias_b, bias)):
                act.dma_start(t[:], src.rearrange("(a f) -> a f", a=1).to_broadcast([P, src.shape[0]])
                              ).then_inc(consts_in, 16)

            act.wait_ge(wproj_in, 16 * 5)
            first_norm(0, range(KT))
            for u in (0, 1, 4, 5, 6, 7):
                evacuate(0, u)
            act.wait_ge(fill_dve, KT + len(BOUNDED) + 1)

            def body(i, att, pre, first, second, third):
                for g in range(GROUPS):
                    if att:
                        exponentials(i, g)
                        if g % 2 and 5 <= g <= 19:
                            copy_context(i, 0, (g - 5) // 2)
                        if g % 2 and g >= 21:
                            copy_context(i, 1, (g - 21) // 2)
                        if g == 18:
                            copy_sums(i, 0)
                        if g == 19:
                            store_sums(i, 0)
                        if g == 21:
                            load_sums(i, 0)
                        if g == 25:
                            store_reciprocals(i, 0)
                        if g == 28:
                            spread_reciprocals(i, 0)
                    if first:
                        if g in (1, 3):
                            copy_context(i - 1, 1, 6 + g // 2)
                        if g == 2:
                            copy_sums(i - 1, 1)
                        if g == 3:
                            store_sums(i - 1, 1)
                        if g == 5:
                            load_sums(i - 1, 1)
                        if g == 9:
                            store_reciprocals(i - 1, 1)
                        if g == 12:
                            spread_reciprocals(i - 1, 1)
                    if pre:
                        if g in (2, 3, 4, 5):
                            first_norm(i + 1, (2 * g - 4, 2 * g - 3))
                        if g in (6, 8, 14, 17, 23, 28):
                            evacuate(i + 1, {6: 0, 8: 1, 14: 4, 17: 5, 23: 6, 28: 7}[g])
                    if second:
                        if g in (9, 10):
                            act.wait_ge(norm_ready[1], 4 * (i - 2) + 4)
                            normalise(1, i - 2, attn, attn, ln2_done, range(4 * (g - 9), 4 * (g - 8)))
                        if g in (23, 24):
                            act.wait_ge(norm_ready[2], 4 * (i - 2) + 4)
                            at_least(act, g_mm, 3 * (i - 2))
                            normalise(2, i - 2, x1, x3, x3_done, range(4 * (g - 23), 4 * (g - 22)))
                        if g == 26:
                            at_least(act, x3T_stored, 16 * (i - 2))
                            at_least(act, g_mm, 3 * (i - 2))
                            copy_turned(i - 2, 0)
                        if g == 31:
                            copy_turned(i - 2, 1)
                    if third and g == 17:
                        act.wait_ge(top_dve, STEPS * (i - 3) + 12)
                        act.activation(ed[:], dm[:], ACT.Exp).then_inc(ed_done, 1)

            iterations(act, body)

            act.wait_ge(product_done, 8 * B)
            act.dma_start(w1_sb, W1).then_inc(moe_w, 16)
            act.dma_start(w2_sb, W2).then_inc(moe_w, 16)
            act.dma_start(b1_c[:], b1).then_inc(moe_w, 16)
            act.dma_start(b2_b, b2.rearrange("(a e) f -> a (e f)", a=1).to_broadcast([P, E * F])).then_inc(moe_w, 16)
            act.wait_ge(clip_done, GROUPS * B)
            act.wait_ge(moe_w, 16 * 4)

            def relus(k, s):
                for e in range(E):
                    H = E * (2 * k + s) + e
                    act.wait_ge(hid_mm, H + 1)
                    at_least(act, y_mm, H - 1)
                    for h in range(NH):
                        act.activation(hidden[:, e % 2, h, :], score_ps[:, e % 2, h, :], ACT.Relu,
                                       bias=b1_c[:, e * NH + h:e * NH + h + 1]).then_inc(hid_done, 1)

            for s in range(2):
                relus(0, s)
            with act.Fori(1, B) as k:
                for s in range(2):
                    relus(k, s)

        @block.vector
        def _(dve):
            def clip(i, g):
                half, kt = g // 16, g % 16 // 2
                G = GROUPS * i + g
                dve.wait_ge(exp_done, G + 1)
                at_least(dve, pv_done, G - 3)
                if kt in ADDED:
                    dve.tensor_scalar(probs[:, g % 4], exps[:, g % 2], E_LO, E_HI, ALU.max, ALU.min
                                      ).then_inc(clip_done, 1)
                else:
                    m = BOUNDED.index(kt)
                    dve.scalar_tensor_tensor(probs[:, g % 4], exps[:, g % 2], E_LO,
                                             clipmask[:, m:m + 1, half * HALF:(half + 1) * HALF].to_broadcast([P, 2, HALF]),
                                             ALU.max, ALU.min).then_inc(clip_done, 1)

            def statistics(n, j, src):
                at_least(dve, norm_ready[n], 4 * j)
                for t in range(KT):
                    ins = dve.bn_stats(st[n][:, t, :], src[:, t, :])
                ins.then_inc(stats[n], 1)
                dve.wait_ge(stats[n], 4 * j + 1)
                s = st[n]
                dve.tensor_tensor(mean2[n][:], s[:, :, 1], s[:, :, 4], ALU.add)
                dve.tensor_tensor(mdif[n][:], s[:, :, 1], s[:, :, 4], ALU.subtract)
                dve.tensor_tensor(vsum[n][:], s[:, :, 2], s[:, :, 5], ALU.add).then_inc(stats[n], 1)
                dve.wait_ge(stats[n], 4 * j + 2)
                dve.scalar_tensor_tensor(mdif2[n][:], mdif[n][:], 0.25, mdif[n][:], ALU.mult, ALU.mult).then_inc(stats[n], 1)
                dve.wait_ge(stats[n], 4 * j + 3)
                dve.scalar_tensor_tensor(var[n][:], vsum[n][:], 1.0 / F, mdif2[n][:], ALU.mult, ALU.add
                                         ).then_inc(stats[n], 1)

            def evacuate(j, u):
                if u < 4:
                    dve.wait_ge(pre_mm, 8 * j + u + 1)
                    at_least(dve, v_in[u - 2], 16 * j)
                    dve.tensor_tensor(vnew[:, 4 * (u - 2):4 * (u - 1), :],
                                      side_ps[:].rearrange("p (t f) -> p t f", t=4),
                                      bv_b[:].unsqueeze(1).to_broadcast([P, 4, F]), ALU.add).then_inc(pre_dve, 1)
                else:
                    half, n = u % 2, u // 2 - 2
                    cols = slice(half * HALF, (half + 1) * HALF)
                    dve.wait_ge(pre_act, 6 * j + u - 1)
                    dve.scalar_tensor_tensor((q_lo, k_lo)[n][:, cols], side_ps[:], (bq_c, bk_c)[n][:, 0:1],
                                             (q_hi, k_hi)[n][:, cols].bitcast(F32),
                                             ALU.add, ALU.subtract).then_inc(pre_dve, 1)

            def turn_over(j, half):
                U = 2 * j + half
                dve.wait_ge(den_in, 16 * (U + 1))
                at_least(dve, rden_stored, 16 * U)
                dve.reciprocal(rden_sq[:], den_sq[:]).then_inc(rden_done, 1)

            def divide_contexts(j, half, n):
                U = 2 * j + half
                if n == 0:
                    dve.wait_ge(rdenB_in, 16 * (U + 1))
                    dve.wait_ge(ctx_out, 8 * (U + 1))
                kts = slice(2 * n, 2 * n + 2)
                dve.tensor_tensor(rdenB[:, kts, :], ctxu[:, KT * half + 2 * n:KT * half + 2 * n + 2, :],
                                  rdenB[:, kts, :], ALU.mult).then_inc(product_done, 1)

            def residual(j, half):
                dve.wait_ge(o_mm, 2 * j + half + 1)
                dve.wait_ge(xnb_done, j + 1)
                at_least(dve, x1_done, 2 * j)
                dve.tensor_tensor(attn[:, 4 * half:4 * half + 4, :], side_ps[:].rearrange("p (t f) -> p t f", t=4),
                                  xnpost[:, 4 * half:4 * half + 4, :], ALU.add).then_inc(o_done, 1)

            def top_step(j, n):
                lanes = lambda v: v[:].unsqueeze(2).to_broadcast([P, KT, E])
                ranks = rank[:].unsqueeze(1).to_broadcast([P, KT, E])
                if n > 1:
                    dve.wait_ge(top_dve, STEPS * j + n - 1)
                if n == 1:
                    dve.wait_ge(g_mm, 3 * j + 3)
                    ins = dve.tensor_tensor(lg[:], side_ps[:, 0:KT * E].rearrange("p (t e) -> p t e", e=E),
                                            gateb[:].unsqueeze(1).to_broadcast([P, KT, E]), ALU.add)
                elif n == 2:
                    ins = dve.tensor_reduce(m1[:], lg[:], AX_X, ALU.max)
                elif n == 3:
                    ins = dve.tensor_tensor(eq[:], lg[:], lanes(m1), ALU.is_equal)
                elif n == 4:
                    ins = dve.tensor_tensor(cand[:], eq[:], ranks, ALU.mult)
                elif n == 5:
                    ins = dve.tensor_reduce(r1[:], cand[:], AX_X, ALU.max)
                elif n == 6:
                    ins = dve.tensor_tensor(oh1[:], ranks, lanes(r1), ALU.is_equal)
                elif n == 7:
                    ins = dve.scalar_tensor_tensor(lg2[:], oh1[:], -FAR, lg[:], ALU.mult, ALU.add)
                elif n == 8:
                    ins = dve.tensor_reduce(m2[:], lg2[:], AX_X, ALU.max)
                elif n == 9:
                    ins = dve.tensor_tensor(eq[:], lg2[:], lanes(m2), ALU.is_equal)
                elif n == 10:
                    ins = dve.tensor_tensor(cand[:], eq[:], ranks, ALU.mult)
                elif n == 11:
                    ins = dve.tensor_reduce(r2[:], cand[:], AX_X, ALU.max)
                elif n == 12:
                    ins = dve.tensor_tensor(dm[:], m2[:], m1[:], ALU.subtract)
                elif n == 13:
                    ins = dve.tensor_tensor(oh2[:], ranks, lanes(r2), ALU.is_equal)
                elif n == 14:
                    dve.wait_ge(ed_done, j + 1)
                    ins = dve.tensor_scalar(es[:], ed[:], 1.0, None, ALU.add)
                elif n == 15:
                    ins = dve.reciprocal(w1st[:], es[:])
                elif n == 16:
                    ins = dve.tensor_tensor(w2nd[:], ed[:], w1st[:], ALU.mult)
                elif n == 17:
                    ins = dve.tensor_tensor(cmb1[:], oh1[:], lanes(w1st), ALU.mult)
                elif n == 18:
                    ins = dve.tensor_tensor(cmb2[:], oh2[:], lanes(w2nd), ALU.mult)
                else:
                    at_least(dve, c_stored, 16 * j)
                    ins = dve.tensor_tensor(comb[:], cmb1[:], cmb2[:], ALU.add)
                ins.then_inc(top_dve, 1)

            dve.wait_ge(xpre_in, 16)

            dve.wait_ge(xpre_in, 16)
            statistics(0, 0, xpre)
            for t in range(KT):
                dve.wait_ge(adj_in, 16 * KT)
                if t in ADDED:
                    dve.tensor_scalar(addmask[:, ADDED.index(t), :], adj_sb[:, t, :].bitcast(I32), 0.0, NO_EDGE,
                                      ALU.is_equal, ALU.mult).then_inc(fill_dve, 1)
                else:
                    dve.tensor_scalar(clipmask[:, BOUNDED.index(t), :], adj_sb[:, t, :].bitcast(I32), 0.0, E_HI,
                                      ALU.not_equal, ALU.mult).then_inc(fill_dve, 1)
            dve.wait_ge(fill_dve, KT)
            for m in range(len(BOUNDED)):
                dve.tensor_scalar(clipmask[:, m, :], clipmask[:, m, :], E_LO, None, ALU.max).then_inc(fill_dve, 1)
            dve.wait_ge(wproj_in, 16 * 5)
            dve.wait_ge(consts_in, 16 * 8)
            dve.tensor_tensor(gateb[:], bg_b[:], bias_b[:], ALU.add).then_inc(fill_dve, 1)
            for u in range(2, 8):
                evacuate(0, u)
            dve.wait_ge(fill_dve, KT + len(BOUNDED) + 1)
            dve.wait_ge(xpre_in, 32)
            statistics(0, 1, xpre)

            def body(i, att, pre, first, second, third):
                for g in range(GROUPS):
                    if att:
                        clip(i, g)
                        if g == 23:
                            turn_over(i, 0)
                    if first:
                        if g in (1, 3, 5, 7):
                            divide_contexts(i - 1, 0, g // 2)
                        if g == 7:
                            turn_over(i - 1, 1)
                        if g == 20:
                            residual(i - 1, 0)
                        if g in (16, 18, 20, 22):
                            divide_contexts(i - 1, 1, g // 2 - 8)
                    if third:
                        if 3 <= g <= 15:
                            top_step(i - 3, g - 2)
                        if 18 <= g <= 23:
                            top_step(i - 3, g - 4)
                    if second:
                        if g == 1:
                            residual(i - 2, 1)
                        if g == 2:
                            dve.wait_ge(o_done, 2 * (i - 2) + 2)
                            statistics(1, i - 2, attn)
                        if g == 21:
                            dve.wait_ge(x1_done, 2 * (i - 2) + 2)
                            statistics(2, i - 2, x1)
                    if pre:
                        if g == 26 and (not isinstance(i, int) or i + 2 < B):
                            dve.wait_ge(xpre_in, 16 * (i + 2) + 16)
                            statistics(0, i + 2, xpre)
                        if g in (9, 11, 15, 17, 23, 28):
                            evacuate(i + 1, {9: 2, 11: 3, 15: 4, 17: 5, 23: 6, 28: 7}[g])

            iterations(dve, body, last=B - 3)

            def combine(k, s):
                dve.wait_ge(chunk_in[s], 48 * k + 48)
                for e in range(E):
                    H = E * (2 * k + s) + e
                    dve.wait_ge(y_mm, H + 1)
                    if e:
                        dve.wait_ge(acc_b, H)
                    for t in range(4):
                        ins = dve.scalar_tensor_tensor(acc[s][:, t * F:(t + 1) * F], ctx_ps[:, e % 2, t * F:(t + 1) * F],
                                                       cch[:, s, t * E + e:t * E + e + 1],
                                                       acc[s][:, t * F:(t + 1) * F], ALU.mult, ALU.add)
                    ins.then_inc(acc_y, 1)
                    dve.wait_ge(acc_y, H + 1)
                    for t in range(4):
                        ins = dve.scalar_tensor_tensor(acc[s][:, t * F:(t + 1) * F], b2_b[:, e * F:(e + 1) * F],
                                                       cch[:, s, t * E + e:t * E + e + 1],
                                                       acc[s][:, t * F:(t + 1) * F], ALU.mult, ALU.add)
                    ins.then_inc(acc_b, 1)

            dve.wait_ge(moe_w, 16 * 4)
            with dve.Fori(0, B) as k:
                for s in range(2):
                    combine(k, s)

        @block.gpsimd
        def _(pool):
            pool.memset(ident[:], 0.0).then_inc(fills, 1)
            pool.memset(onehot[:], 0.0).then_inc(fills, 1)
            pool.memset(eps8[:], EPS).then_inc(fills, 1)
            pool.memset(mhalf8[:], -0.5).then_inc(fills, 1)
            pool.iota(rank[:], pattern=[[-1, E]], base=E, channel_multiplier=0,
                      allow_small_or_imprecise_dtypes=True).then_inc(fills, 1)
            pool.wait_ge(fills, 5)
            pool.affine_select(out=ident[:], in_=ident[:], compare_op=ALU.not_equal, fill=1.0, base=0,
                               pattern=[[-1, P]], channel_multiplier=1).then_inc(fills, 2)
            for t in range(KT):
                pool.memset(onehot[:, t, t:t + 1], 1.0).then_inc(fills, 1)
            pool.wait_ge(fills, 7 + KT)
            pool.tensor_copy(ident16[:], ident[:]).then_inc(fills, 1)

            def scale_and_shift(n, j, used):
                pool.wait_ge(stats[n], 4 * j + 4)
                at_least(pool, used, KT * j)
                pool.tensor_tensor(veps[n][:], var[n][:], eps8[:], ALU.add).then_inc(norm_ready[n], 1)
                pool.wait_ge(norm_ready[n], 4 * j + 1)
                pool.tensor_tensor(rstd[n][:], veps[n][:], mhalf8[:], ALU.pow).then_inc(norm_ready[n], 1)
                pool.wait_ge(norm_ready[n], 4 * j + 2)
                pool.tensor_tensor(nm[n][:], mean2[n][:], rstd[n][:], ALU.mult).then_inc(norm_ready[n], 1)
                pool.wait_ge(norm_ready[n], 4 * j + 3)
                pool.tensor_tensor(shift[n][:], nm[n][:], mhalf8[:], ALU.mult).then_inc(norm_ready[n], 1)

            pool.wait_ge(fills, 8 + KT)
            scale_and_shift(0, 0, xn_done)
            scale_and_shift(0, 1, xn_done)
            pool.wait_ge(consts_in, 16 * 8)

            def sum_key_tiles(j, half):
                U = 2 * j + half
                pool.wait_ge(product_done, 4 * (U + 1))
                pool.tensor_tensor(rdenB[:, 0:4, :], rdenB[:, 0:4, :], rdenB[:, 4:8, :], ALU.add).then_inc(sum_done, 1)
                pool.wait_ge(sum_done, 3 * U + 1)
                pool.tensor_tensor(rdenB[:, 0:2, :], rdenB[:, 0:2, :], rdenB[:, 2:4, :], ALU.add).then_inc(sum_done, 1)
                pool.wait_ge(sum_done, 3 * U + 2)
                at_least(pool, o_mm, 2 * (j - 1) + half + 1)
                pool.tensor_tensor(ctxn[:, half * HALF:(half + 1) * HALF], rdenB[:, 0, :], rdenB[:, 1, :], ALU.add
                                   ).then_inc(sum_done, 1)

            def body(i, att, pre, first, second, third):
                wide = lambda v: v[:].unsqueeze(1).to_broadcast([P, KT, F])
                if second:
                    scale_and_shift(1, i - 2, ln2_done)
                if first:
                    sum_key_tiles(i - 1, 0)
                    pool.wait_ge(post_in, 16 * (i - 1) + 16)
                    pool.tensor_tensor(xnpost[:], xnpost[:], wide(bo_b), ALU.add).then_inc(xnb_done, 1)
                if second:
                    pool.wait_ge(ln2_done, KT * (i - 2) + KT)
                    pool.tensor_tensor(attn[:], attn[:], wide(gamma_b), ALU.mult).then_inc(x1_done, 1)
                    pool.wait_ge(x1_done, 2 * (i - 2) + 1)
                    pool.wait_ge(xpb_done, (i - 2) + 1)
                    at_least(pool, x3_done, KT * (i - 2))
                    at_least(pool, x1_stored, 16 * (i - 2))
                    pool.tensor_tensor(x1[:], attn[:], xpost[:], ALU.add).then_inc(x1_done, 1)
                    scale_and_shift(2, i - 2, x3_done)
                if first:
                    pool.wait_ge(xpost_in, 16 * (i - 1) + 16)
                    pool.tensor_tensor(xpost[:], xpost[:], wide(beta_b), ALU.add).then_inc(xpb_done, 1)
                if first:
                    sum_key_tiles(i - 1, 1)
                if pre and (not isinstance(i, int) or i + 2 < B):
                    scale_and_shift(0, i + 2, xn_done)

            iterations(pool, body, last=B - 3)



_INS = ["x", "adjT", "WqT", "WkT", "WvT", "WoT", "bq", "bk", "bv", "bo", "gamma", "beta",
        "Wg", "bg", "bias", "W1", "b1", "W2", "b2"]


def kernel(x, adj, L0_gnn_Wq, L0_gnn_bq, L0_gnn_Wk, L0_gnn_bk, L0_gnn_Wv, L0_gnn_bv, L0_gnn_Wo, L0_gnn_bo,
           L0_gnn_gamma, L0_gnn_beta, L0_ffn_Wg, L0_ffn_bg, L0_ffn_bias, L0_ffn_W1, L0_ffn_b1, L0_ffn_W2, L0_ffn_b2):
    import concourse.bacc as bacc
    from concourse.bass_utils import run_bass_kernel_spmd

    B, N, F = x.shape
    E, _, HID = L0_ffn_W1.shape
    KT, NH = N // P, HID // P
    flat = lambda a: np.ascontiguousarray(np.asarray(a))
    laid = {
        "x": flat(np.asarray(x).reshape(B, KT, P, F).transpose(0, 2, 1, 3).reshape(B, P, KT * F)),
        "adjT": flat(np.asarray(adj).T),
        "WqT": flat(np.asarray(L0_gnn_Wq).T), "WkT": flat(np.asarray(L0_gnn_Wk).T),
        "WvT": flat(np.asarray(L0_gnn_Wv).T), "WoT": flat(np.asarray(L0_gnn_Wo).T),
        "bq": flat(L0_gnn_bq), "bk": flat(L0_gnn_bk), "bv": flat(L0_gnn_bv), "bo": flat(L0_gnn_bo),
        "gamma": flat(L0_gnn_gamma), "beta": flat(L0_gnn_beta),
        "Wg": flat(L0_ffn_Wg), "bg": flat(L0_ffn_bg), "bias": flat(L0_ffn_bias),
        "W1": flat(np.asarray(L0_ffn_W1).transpose(1, 0, 2).reshape(F, E * HID)),
        "b1": flat(np.asarray(L0_ffn_b1).reshape(E * NH, P).T),
        "W2": flat(np.asarray(L0_ffn_W2).reshape(E * NH, P, F).transpose(1, 0, 2).reshape(P, E * NH * F)),
        "b2": flat(L0_ffn_b2),
    }
    nc = bacc.Bacc("TRN2", target_bir_lowering=False, num_devices=1)
    args = [nc.dram_tensor(f"in_{n}", laid[n].shape, mybir.dt.from_np(laid[n].dtype), kind="ExternalInput").ap()
            for n in _INS]
    out = nc.dram_tensor("out_0", (B, P, KT * F), F32, kind="ExternalOutput").ap()
    gnn_moe_kernel(nc, *args, out)
    got = run_bass_kernel_spmd(nc, [{f"in_{n}": laid[n] for n in _INS}], core_ids=[0]).results[0]["out_0"]
    return np.ascontiguousarray(got.reshape(B, P, KT, F).transpose(0, 2, 1, 3).reshape(B, N, F))
```

```python
from contextlib import ExitStack

import numpy as np

import concourse.bass as bass
from concourse import mybir

F32 = mybir.dt.float32
F32R = mybir.dt.float32r
BF16 = mybir.dt.bfloat16
I32 = mybir.dt.int32
ALU = mybir.AluOpType
ACT = mybir.ActivationFunctionType
AX_X = mybir.AxisListType.X

P = 128
HEADS = 4
DH = P // HEADS
GROUPS = 32
LAG = 3
EPS = 1e-5
E_HI = float(np.exp(np.float32(10.0)))
E_LO = float(np.exp(np.float32(-10.0)))
FAR = 1.0e30
NO_EDGE = -float(2.0 ** 60)
ADDED = (0, 2, 4, 6)
BOUNDED = (1, 3, 5, 7)
STEPS = 19
TILE = 512
RANKS = 10


def at_least(eng, sem, value):
    if isinstance(value, int) and value <= 0:
        return
    eng.wait_ge(sem, value)


def gnn_moe_kernel(nc, x, adjT, WqT, WkT, WvT, WoT, bq, bk, bv, bo, gamma, beta,
                   Wg, bg, bias, W1, b1, W2, b2, out):
    B, N, F = x.shape[0], adjT.shape[0], WqT.shape[0]
    KT = N // P
    HALF = N // 2
    E = Wg.shape[1]
    HID = W1.shape[2]
    NH = HID // P
    T = B * N
    REC = F + 2 * E
    REGION = T + TILE
    TILES = 2 * T // TILE + E
    AREAS = 2 * E
    SCALE = float(1.0 / np.sqrt(np.float32(DH)))

    ctx = ExitStack()
    with ctx:
        def sb(name, shape, dt=F32):
            return ctx.enter_context(nc.sbuf_tensor(name, shape, dt))

        def ps(name, shape, dt=F32):
            return ctx.enter_context(nc.psum_tensor(name, shape, dt))

        def sem(name):
            return ctx.enter_context(nc.semaphore(name))

        xn_dram = nc.dram_tensor("xn_scratch", [B, P, KT * F], F32, kind="Internal").ap()
        x1_dram = nc.dram_tensor("x1_scratch", [B, P, KT * F], F32, kind="Internal").ap()
        x3_dram = nc.dram_tensor("x3_scratch", [B, P, KT * F], F32, kind="Internal").ap()
        rec_dram = nc.dram_tensor("rec_scratch", [E * REGION + E * TILE, REC], F32, kind="Internal").ap()
        y_dram = nc.dram_tensor("y_scratch", [2 * T + AREAS * TILE, F], F32, kind="Internal").ap()
        pick_dram = nc.dram_tensor("pick_scratch", [TILES, E], F32, kind="Internal").ap()
        q_dram, k_dram = (nc.dram_tensor(f"{n}_scratch", [4, DH, HEADS, N], F32, kind="Internal").ap() for n in "qk")
        den_dram = nc.dram_tensor("den_scratch", [HEADS, KT, HALF], F32, kind="Internal").ap()
        rden_dram = nc.dram_tensor("rden_scratch", [HEADS, KT, HALF], F32, kind="Internal").ap()

        score_ps = ps("score_ps", [P, 2, 2, HALF])
        ctx_ps = ps("ctx_ps", [P, 2, HALF])
        den_ps = ps("den_ps", [P, HALF])
        side_ps = ps("side_ps", [P, 512])

        addmask = sb("addmask", [P, len(ADDED), N], BF16)
        clipmask = sb("clipmask", [P, len(BOUNDED), N])
        kstack = sb("kstack", [P, HEADS, N], F32R)
        qstack = sb("qstack", [P, HEADS, N], F32R)
        vfull = sb("vfull", [P, KT, F])
        exps = sb("exps", [P, 2, 2, HALF])
        probs = sb("probs", [P, 4, 2, HALF])
        ctxu = sb("ctxu", [P, 2 * KT, HALF])
        rdenB = sb("rdenB", [P, KT, HALF])
        den = sb("den", [P, HALF])
        den_sq, rden_sq = sb("den_sq", [P, P]), sb("rden_sq", [P, P])
        xpre = sb("xpre", [P, KT, F])
        xn = sb("xn", [P, KT, F])
        xnT = sb("xnT", [P, N])
        q_hi, q_lo = (sb(n, [P, N], F32R) for n in ("q_hi", "q_lo"))
        k_hi, k_lo = (sb(n, [P, HALF], F32R) for n in ("k_hi", "k_lo"))
        vnew = sb("vnew", [P, KT, F])
        ctxn = sb("ctxn", [P, N])
        xnpost, xpost = sb("xnpost", [P, KT, F]), sb("xpost", [P, KT, F])
        attn = sb("attn", [P, KT, F])
        x1 = sb("x1", [P, KT, F])
        x3 = sb("x3", [P, KT, F])
        x3T = sb("x3T", [P, N])
        wq, wk, wv, wo = (sb(f"w{n}_sb", [P, F]) for n in "qkvo")
        bq_c, bk_c = sb("bq_c", [P, 1]), sb("bk_c", [P, 1])
        bv_b, bo_b, gamma_b, beta_b = (sb(f"{n}_b", [P, F]) for n in ("bv", "bo", "gamma", "beta"))
        wg_sb = sb("wg_sb", [P, E])
        bg_b, bias_b, gateb = sb("bg_b", [P, E]), sb("bias_b", [P, E]), sb("gateb", [P, E])
        ident = sb("ident", [P, P])
        ident16 = sb("ident16", [P, P], BF16)
        onehot = sb("onehot", [P, KT, DH])
        eps8, mhalf8 = sb("eps8", [P, KT]), sb("mhalf8", [P, KT])
        rank = sb("rank", [P, E])
        st = [sb(f"st{n}", [P, KT, 6]) for n in range(3)]
        mean2, mdif, vsum, mdif2, var = ([sb(f"{v}{n}", [P, KT]) for n in range(3)]
                                         for v in ("mean2_", "mdif_", "vsum_", "mdif2_", "var_"))
        veps = [sb(f"veps{n}", [P, KT]) for n in range(3)]
        rstd = [sb(f"rstd{n}", [P, KT]) for n in range(3)]
        nm = [sb(f"nm{n}", [P, KT]) for n in range(3)]
        shift = [sb(f"shift{n}", [P, KT]) for n in range(3)]
        lg, lg2, eq, cand = (sb(n, [P, KT, E]) for n in ("lg", "lg2", "eq", "cand"))
        oh1, oh2, cmb1, cmb2, comb = (sb(n, [P, KT, E]) for n in ("oh1", "oh2", "cmb1", "cmb2", "comb"))
        m1, m2, r1, r2, dm, ed, es, w1st, w2nd = (sb(n, [P, KT]) for n in
                                                  ("m1", "m2", "r1", "r2", "dm", "ed", "es", "w1st", "w2nd"))
        tri, ones = sb("tri", [P, P]), sb("ones", [P, P])
        chosen = sb("chosen", [P, KT, E])
        before = sb("before", [P, KT + 1, E])
        slot = sb("slot", [P, KT, E])
        in1, in2 = cmb1, cmb2
        slot_f, slot_i = sb("slot_f", [P, 2, KT]), sb("slot_i", [P, 2, KT], I32)
        region0 = sb("region0", [P, E])
        token = sb("token", [P, KT])
        rec = sb("rec", [P, KT, REC])

        adj_sb = ctxu[:].rearrange("p (t a) n -> p t (a n)", a=2)
        idle_fill = rdenB[:, 0:2, :].rearrange("p s n -> p (s n)")[:, 0:4 * REC].rearrange("p (a r) -> p a r", a=4)

        room = ctxu[:].rearrange("p s n -> p (s n)")
        taken = [0]

        def part(*shape):
            size = int(np.prod(shape))
            at = taken[0]
            taken[0] += size
            assert taken[0] <= room.shape[1]
            v = room[:, at:at + size]
            return v if len(shape) == 1 else v.rearrange("p (a b) -> p a b", a=shape[0])

        w1_t, w2_t = [part(HID) for _ in range(4)], [part(NH * F) for _ in range(4)]
        b1_t, b2_t = [part(NH) for _ in range(4)], [part(F) for _ in range(4)]
        pick2_t = [part(2 * E) for _ in range(4)]
        rec_t = [part(4, REC) for _ in range(4)]
        xT_t = [part(TILE) for _ in range(2)]
        y_t = [part(4, F) for _ in range(4)]
        picked = [part(4, 2 * E) for _ in range(2)]
        wd_t = [part(4, 2) for _ in range(2)]
        row_t = [part(4).bitcast(I32) for _ in range(4)]
        room, taken[0] = rdenB[:].rearrange("p s n -> p (s n)"), 0
        tail_fill = part(4, REC)
        hidden = exps
        total, tiles_of, upto, step_of, tail_f = (part(E) for _ in range(5))
        tail_i = part(E).bitcast(I32)
        bounds = part(T // TILE)
        more = part(E, T // TILE)
        reached, weighed, pick = part(TILES, E), part(TILES, E), part(TILES, E)
        index_e = part(E)
        index_t, start_f, expert_f, beyond = (part(TILES) for _ in range(4))
        start_i, expert_i = (part(TILES).bitcast(I32) for _ in range(2))
        x1_all = [(kstack, qstack)[j // 4][:, j % 4, :].bitcast(F32) for j in range(B)]
        y_1st = [probs[:, s].rearrange("p h n -> p (h n)") for s in range(4)]
        y_2nd = ([exps[:, s].rearrange("p h n -> p (h n)") for s in range(2)]
                 + [v[:].rearrange("p t f -> p (t f)") for v in (xnpost, xpost)])

        consts_in = sem("consts_in")
        wproj_in = sem("wproj_in")
        adj_in = sem("adj_in")
        fills = sem("fills")
        fill_dve = sem("fill_dve")
        xpre_in = sem("xpre_in")
        stats = [sem(f"stats{n}") for n in range(3)]
        norm_ready = [sem(f"norm_ready{n}") for n in range(3)]
        xn_done = sem("xn_done")
        xn_stored = sem("xn_stored")
        pre_mm = sem("pre_mm")
        pre_act = sem("pre_act")
        pre_dve = sem("pre_dve")
        q_stored = [sem(f"q_stored{c}") for c in range(2)]
        k_stored = [sem(f"k_stored{c}") for c in range(2)]
        q_in = [sem(f"q_in{c}") for c in range(2)]
        k_in = [sem(f"k_in{c}") for c in range(2)]
        v_in = [sem(f"v_in{c}") for c in range(2)]
        qk_done = sem("qk_done")
        exp_done = sem("exp_done")
        clip_done = sem("clip_done")
        pv_done = sem("pv_done")
        ctx_out = sem("ctx_out")
        den_out = sem("den_out")
        den_stored = sem("den_stored")
        den_in = sem("den_in")
        rden_done = sem("rden_done")
        rden_stored = sem("rden_stored")
        rdenB_in = sem("rdenB_in")
        product_done = sem("product_done")
        sum_done = sem("sum_done")
        last_sum = sem("last_sum")
        post_in = sem("post_in")
        xpost_in = sem("xpost_in")
        xnb_done = sem("xnb_done")
        xpb_done = sem("xpb_done")
        o_mm = sem("o_mm")
        o_done = sem("o_done")
        ln2_done = sem("ln2_done")
        x1_done = sem("x1_done")
        x1_stored = sem("x1_stored")
        x3_done = sem("x3_done")
        g_mm = sem("g_mm")
        x3T_done = sem("x3T_done")
        x3_stored = sem("x3_stored")
        top_dve = sem("top_dve")
        ed_done = sem("ed_done")
        count_dve = sem("count_dve")
        rank_mm = sem("rank_mm")
        slot_dve = sem("slot_dve")
        rec_in = sem("rec_in")
        rec_stored = sem("rec_stored")
        idle_made = sem("idle_made")
        idle_stored = sem("idle_stored")

        tail_made = sem("tail_made")
        table_dve = sem("table_dve")
        tail_stored = sem("tail_stored")
        pick_stored = sem("pick_stored")
        tile_in = [sem(f"tile_in{u}") for u in range(4)]
        rec_t_in = [sem(f"rec_t_in{u}") for u in range(4)]
        xT_mm = sem("xT_mm")
        xT_done = sem("xT_done")
        hid_mm = sem("hid_mm")
        hid_done = sem("hid_done")
        y_mm = sem("y_mm")
        picked_done = sem("picked_done")
        y_dve = sem("y_dve")
        y_stored = [sem(f"y_stored{u}") for u in range(4)]
        x1_in = sem("x1_in")
        sum_in = [sem(f"sum_in{s}") for s in range(4)]
        sum_dve = sem("sum_dve")
        out_stored = [sem(f"out_stored{s}") for s in range(4)]

        def wait_sum(eng, j, half):
            if isinstance(j, int) and j == B - 1:
                eng.wait_ge(last_sum, 3 * half + 3)
            else:
                eng.wait_ge(sum_done, 3 * (2 * j + half) + 3)

        def back(k, u, n):
            return (k, u - n) if u >= n else (k - 1, u - n + 4)

        FILLS = 12 + KT
        TABLE = 10 + E
        block = ctx.enter_context(nc.Block())

        def iterations(eng, body, last=B - 2):
            def step(i):
                body(i, att=i < B, pre=i + 1 < B, first=1 <= i <= B, second=2 <= i <= B + 1,
                     third=3 <= i <= B + 2, fourth=i >= 4)

            for i in range(5):
                step(i)
            with eng.Fori(5, last + 1) as i:
                body(i, att=True, pre=True, first=True, second=True, third=True, fourth=True)
            for i in range(last + 1, B + 4):
                step(i)

        @block.sync
        def _(sp):
            def load_xpre(j):
                at_least(sp, xn_done, KT * j)
                sp.dma_start(xpre[:].rearrange("p t f -> p (t f)"),
                             x[bass.ds(j, 1)].rearrange("a p n -> p (a n)")).then_inc(xpre_in, 16)

            def store_parts(j, half, n):
                sp.wait_ge(pre_dve, 6 * j + 3 + 2 * n + half)
                cols = slice(half * HALF, (half + 1) * HALF)
                for row, src in enumerate(((q_hi, q_lo, q_hi, q_lo), (k_hi, k_hi, k_lo, k_lo))[n]):
                    sp.dma_start((q_dram, k_dram)[n][row, :, :, cols].rearrange("d h n -> h d n"),
                                 src[:, cols if n == 0 else slice(None)].bitcast(F32)).then_inc((q_stored, k_stored)[n][half], 16)

            def stack_q(j, half):
                sp.wait_ge(q_stored[half], 64 * j + 64)
                cols = slice(half * HALF, (half + 1) * HALF)
                sp.dma_start(qstack[:, :, cols].bitcast(F32),
                             q_dram[:, :, :, cols].rearrange("r d h n -> (r d) h n")).then_inc(q_in[half], 16)

            def stack_k(j, half):
                sp.wait_ge(k_stored[half], 64 * j + 64)
                cols = slice(half * HALF, (half + 1) * HALF)
                sp.dma_start(kstack[:, :, cols].bitcast(F32),
                             k_dram[:, :, :, cols].rearrange("r d h n -> (r d) h n")).then_inc(k_in[half], 16)

            def hand_v(j, half):
                at_least(sp, pv_done, GROUPS * (j - 1) + 24 + 8 * half)
                sp.dma_start(vfull[:, 4 * half:4 * half + 4, :], vnew[:, 4 * half:4 * half + 4, :]).then_inc(v_in[half], 16)

            def store_xn(j):
                sp.wait_ge(xn_done, KT * j + KT)
                sp.dma_start(xn_dram[bass.ds(j, 1)].rearrange("a p n -> p (a n)"),
                             xn[:].rearrange("p t f -> p (t f)")).then_inc(xn_stored, 16)

            sp.dma_start(xpre[:].rearrange("p t f -> p (t f)"),
                         x[0:1].rearrange("a p n -> p (a n)")).then_inc(xpre_in, 16)
            for w, src in ((wq, WqT), (wk, WkT), (wv, WvT)):
                sp.dma_start(w[:], src).then_inc(wproj_in, 16)
            for c, src in ((bq_c, bq), (bk_c, bk)):
                sp.dma_start(c[:], src.rearrange("(p a) -> p a", a=1)).then_inc(wproj_in, 16)
            for t in range(KT):
                sp.dma_start(adj_sb[:, t, :].bitcast(I32), adjT[t * P:(t + 1) * P, :]).then_inc(adj_in, 16)

            store_xn(0)
            load_xpre(1)
            store_parts(0, 0, 0)
            store_parts(0, 1, 0)
            stack_q(0, 0)
            store_parts(0, 0, 1)
            stack_k(0, 0)
            store_parts(0, 1, 1)
            hand_v(0, 0)
            sp.wait_ge(idle_made, 2)
            for e in range(E):
                first_row = E * REGION + e * TILE
                sp.dma_start(rec_dram[first_row:first_row + TILE].rearrange("(a p) r -> p a r", p=P), idle_fill
                             ).then_inc(idle_stored, 16)

            def body(i, att, pre, first, second, third, fourth):
                if att:
                    hand_v(i, 1)
                    stack_k(i, 1)
                    stack_q(i, 1)
                if first:
                    if second:
                        sp.wait_ge(o_done, 2 * (i - 2) + 2)
                    sp.wait_ge(xn_stored, 16 * (i - 1) + 16)
                    sp.dma_start(xnpost[:].rearrange("p t f -> p (t f)"),
                                 xn_dram[bass.ds(i - 1, 1)].rearrange("a p n -> p (a n)")).then_inc(post_in, 16)
                if pre:
                    store_xn(i + 1)
                    if not isinstance(i, int) or i + 2 < B:
                        load_xpre(i + 2)
                    store_parts(i + 1, 0, 0)
                    stack_q(i + 1, 0)
                    store_parts(i + 1, 1, 0)
                if second:
                    sp.wait_ge(x1_done, 2 * (i - 2) + 2)
                    sp.dma_start(x1_dram[bass.ds(i - 2, 1)].rearrange("a p n -> p (a n)"),
                                 x1[:].rearrange("p t f -> p (t f)")).then_inc(x1_stored, 16)
                if first:
                    sp.dma_start(xpost[:].rearrange("p t f -> p (t f)"),
                                 x[bass.ds(i - 1, 1)].rearrange("a p n -> p (a n)")).then_inc(xpost_in, 16)
                if pre:
                    store_parts(i + 1, 0, 1)
                    stack_k(i + 1, 0)
                    hand_v(i + 1, 0)
                if second:
                    sp.wait_ge(x3_done, KT * (i - 2) + KT)
                    sp.dma_start(x3_dram[bass.ds(i - 2, 1)].rearrange("a p n -> p (a n)"),
                                 x3[:].rearrange("p t f -> p (t f)")).then_inc(x3_stored, 16)
                if pre:
                    store_parts(i + 1, 1, 1)

            iterations(sp, body, last=B - 3)

            sp.wait_ge(x1_stored, 16 * B)
            sp.wait_ge(idle_stored, 16 * E)

            sp.wait_ge(tail_made, 2)
            sp.wait_ge(table_dve, TABLE)
            sp.dma_start(pick_dram.rearrange("(a t) e -> a (t e)", a=1),
                         pick.rearrange("p t e -> p (t e)")[0:1]).then_inc(pick_stored, 16)
            for e in range(E):
                row = nc.values_load(tail_i[0:1, e:e + 1], engines=[mybir.EngineType.SP],
                                     min_val=e * REGION, max_val=e * REGION + T)
                sp.dma_start(rec_dram[bass.ds(row, TILE)].rearrange("(a p) r -> p a r", p=P), tail_fill
                             ).then_inc(tail_stored, 16)
            sp.wait_ge(pick_stored, 16)

            def load_weights(k, u):
                t = 4 * k + u
                e = nc.values_load(expert_i[0:1, bass.ds(t, 1)], engines=[mybir.EngineType.SP], min_val=0, max_val=E - 1)
                at_least(sp, y_dve, 16 * k + 4 * u - 12)
                sp.dma_start(w1_t[u], W1[bass.ds(e, 1)].rearrange("a p n -> p (a n)")).then_inc(tile_in[u], 16)
                sp.dma_start(w2_t[u], W2[bass.ds(e, 1)].rearrange("a p n -> p (a n)")).then_inc(tile_in[u], 16)
                sp.dma_start(b1_t[u], b1[bass.ds(e, 1)].rearrange("a p n -> p (a n)")).then_inc(tile_in[u], 16)
                sp.dma_start(b2_t[u], b2[bass.ds(e, 1)].to_broadcast([P, F])).then_inc(tile_in[u], 16)

            def load_records(k, u):
                t = 4 * k + u
                row = nc.values_load(start_i[0:1, bass.ds(t, 1)], engines=[mybir.EngineType.SP],
                                     min_val=0, max_val=E * REGION + (E - 1) * TILE)
                if isinstance(k, int):
                    at_least(sp, xT_mm, t - 3)
                at_least(sp, picked_done, t - 3)
                sp.dma_start(rec_t[u], rec_dram[bass.ds(row, TILE)].rearrange("(a p) r -> p a r", p=P)).then_inc(rec_t_in[u], 16)
                sp.dma_start(pick2_t[u].rearrange("p (c e) -> p c e", e=E),
                             pick_dram[bass.ds(t, 1)].unsqueeze(1).to_broadcast([P, 2, E])).then_inc(rec_t_in[u], 16)

            load_weights(0, 0)
            sp.wait_ge(tail_stored, 16 * E)
            sp.wait_ge(rec_stored, 32 * KT * B)
            load_records(0, 0)
            for u in range(1, 4):
                load_weights(0, u)
                load_records(0, u)
            for u in range(4):
                load_records(1, u)
                load_weights(1, u)
            with sp.Fori(2, TILES // 4) as k:
                for u in range(4):
                    load_records(k, u)
                    load_weights(k, u)

            sp.wait_ge(qk_done, GROUPS * B)
            for j in range(B):
                sp.dma_start(x1_all[j], x1_dram[j]).then_inc(x1_in, 16)
            sp.wait_ge(y_mm, TILES)
            for u in range(4):
                sp.wait_ge(y_stored[u], 64 * (TILES // 4))
            for j in range(B):
                if j >= 4:
                    sp.wait_ge(out_stored[j % 4], 16 * (j // 4))
                for c, y in enumerate((y_1st[j % 4], y_2nd[j % 4])):
                    at = j * N + c * T
                    sp.dma_start(y.rearrange("p (t f) -> p t f", f=F),
                                 y_dram[at:at + N].rearrange("(t p) f -> p t f", p=P)).then_inc(sum_in[j % 4], 16)

        @block.tensor
        def _(pe):
            def scores(i, g):
                half, kt, pair = g // 16, g % 16 // 2, g % 2
                cols = slice(half * HALF, (half + 1) * HALF)
                if g in (0, 16):
                    pe.wait_ge(q_in[half], 16 * (i + 1))
                if g in (0, 8):
                    pe.wait_ge(k_in[g // 8], 16 * (i + 1))
                at_least(pe, exp_done, GROUPS * i + g - 1)
                for hh in range(2):
                    mm = pe.matmul(score_ps[:, g % 2, hh, :], kstack[:, 2 * pair + hh, kt * P:(kt + 1) * P],
                                   qstack[:, 2 * pair + hh, cols], start=True, stop=kt in BOUNDED)
                    if kt in ADDED:
                        mm = pe.matmul(score_ps[:, g % 2, hh, :], ident16[:], addmask[:, ADDED.index(kt), cols],
                                       start=False, stop=True)
                mm.then_inc(qk_done, 1)

            def context(i, g):
                half, kt, pair = g // 16, g % 16 // 2, g % 2
                if g in (0, 8):
                    pe.wait_ge(v_in[g // 8], 16 * (i + 1))
                pe.wait_ge(clip_done, GROUPS * i + g + 1)
                if pair == 0:
                    at_least(pe, ctx_out, 16 * i + 8 * half + kt - 1)
                for hh in range(2):
                    c = 64 * pair + DH * hh
                    pe.matmul(ctx_ps[c:c + DH, kt % 2, :], vfull[:, kt, c:c + DH],
                              probs[:, g % 4, hh, :], start=True, stop=True)
                if g % 16 == 0:
                    at_least(pe, den_out, 2 * i + half)
                for hh in range(2):
                    c = 64 * (1 - pair) + DH * hh
                    mm = pe.matmul(den_ps[c:c + DH, :], onehot[:, kt, :], probs[:, g % 4, hh, :],
                                   start=(kt == 0), stop=(kt == KT - 1))
                mm.then_inc(pv_done, 1)

            def prepare(j, u):
                if u < 2:
                    pe.wait_ge(xn_done, KT * j + 4 * u + 4)
                    for t in range(4):
                        mm = pe.transpose(side_ps[:, t * P:(t + 1) * P], xn[:, 4 * u + t, :], ident[:])
                elif u < 4:
                    for t in range(4):
                        tile = 4 * (u - 2) + t
                        mm = pe.matmul(side_ps[:, t * P:(t + 1) * P], xnT[:, tile * P:(tile + 1) * P], wv[:],
                                       start=True, stop=True)
                else:
                    half = u % 2
                    mm = pe.matmul(side_ps[:], (wq, wk)[u // 2 - 2][:], xnT[:, half * HALF:(half + 1) * HALF],
                                   start=True, stop=True)
                mm.then_inc(pre_mm, 1)

            def before_prepare(j, u):
                if u == 0:
                    at_least(pe, pre_dve, 6 * j)
                elif u <= 2:
                    pe.wait_ge(pre_act, 6 * j + u)
                else:
                    pe.wait_ge(pre_dve, 6 * j + u - 2)

            def project(j, half):
                wait_sum(pe, j, half)
                for t in range(4):
                    tile = 4 * half + t
                    mm = pe.matmul(side_ps[:, t * P:(t + 1) * P], ctxn[:, tile * P:(tile + 1) * P], wo[:],
                                   start=True, stop=True)
                mm.then_inc(o_mm, 1)

            def turn_x3(j, half):
                pe.wait_ge(x3_done, KT * j + 4 * half + 4)
                for t in range(4):
                    mm = pe.transpose(side_ps[:, t * P:(t + 1) * P], x3[:, 4 * half + t, :], ident[:])
                mm.then_inc(g_mm, 1)

            def logits(j):
                pe.wait_ge(x3T_done, 2 * j + 2)
                for t in range(KT):
                    mm = pe.matmul(side_ps[:, t * E:(t + 1) * E], x3T[:, t * P:(t + 1) * P], wg_sb[:],
                                   start=True, stop=True)
                mm.then_inc(g_mm, 1)

            def ranks(j):
                pe.wait_ge(count_dve, RANKS * j + RANKS)
                pe.matmul(side_ps[:, KT * E:2 * KT * E], tri[:], chosen[:].rearrange("p t e -> p (t e)"),
                          start=True, stop=False)
                pe.matmul(side_ps[:, KT * E:2 * KT * E], ones[:], before[:, 0:KT, :].rearrange("p t e -> p (t e)"),
                          start=False, stop=True).then_inc(rank_mm, 1)

            pe.wait_ge(fills, FILLS)
            pe.wait_ge(wproj_in, 16 * 5)
            for u in range(8):
                before_prepare(0, u)
                prepare(0, u)
            pe.wait_ge(fill_dve, KT + len(BOUNDED) + 1)

            def body(i, att, pre, first, second, third, fourth):
                for g in range(GROUPS):
                    if att:
                        scores(i, g)
                    if g >= LAG and att:
                        context(i, g - LAG)
                    if g < LAG and first:
                        context(i - 1, GROUPS + g - LAG)
                    if g == 1 and (third or fourth):
                        if third:
                            pe.wait_ge(x3T_done, 2 * (i - 3) + 2)
                            logits(i - 3)
                        if fourth:
                            ranks(i - 4)
                    if g == 3 and second:
                        if third:
                            pe.wait_ge(top_dve, STEPS * (i - 3) + 1)
                        else:
                            pe.wait_ge(pre_dve, 6 * i + 6)
                        project(i - 2, 1)
                    if pre and g in (6, 8, 10, 12, 14, 17):
                        u = (6, 8, 10, 12, 14, 17).index(g)
                        if u > 0:
                            before_prepare(i + 1, u)
                        elif second:
                            pe.wait_ge(o_done, 2 * (i - 2) + 2)
                        else:
                            before_prepare(i + 1, 0)
                        prepare(i + 1, u)
                    if g == 20 and first:
                        if isinstance(i, int) and i == 1:
                            pe.wait_ge(consts_in, 16 * 8)
                        if pre:
                            pe.wait_ge(pre_dve, 6 * (i + 1) + 4)
                        else:
                            pe.wait_ge(o_done, 2 * (i - 2) + 2)
                        project(i - 1, 0)
                    if g == 23 and pre:
                        if first:
                            pe.wait_ge(o_done, 2 * (i - 1) + 1)
                        else:
                            before_prepare(i + 1, 6)
                        prepare(i + 1, 6)
                    if g == 26 and second:
                        if pre:
                            pe.wait_ge(pre_dve, 6 * (i + 1) + 5)
                        elif first:
                            pe.wait_ge(o_done, 2 * (i - 1) + 1)
                        else:
                            pe.wait_ge(o_done, 2 * (i - 2) + 2)
                        turn_x3(i - 2, 0)
                    if g == 28 and pre:
                        if second:
                            pe.wait_ge(x3T_done, 2 * (i - 2) + 1)
                        else:
                            before_prepare(i + 1, 7)
                        prepare(i + 1, 7)
                    if g == 31 and second:
                        if pre:
                            pe.wait_ge(pre_dve, 6 * (i + 1) + 6)
                        else:
                            pe.wait_ge(x3T_done, 2 * (i - 2) + 1)
                        turn_x3(i - 2, 1)

            iterations(pe, body)

            pe.wait_ge(slot_dve, 6 * (B - 1) + 1)
            pe.matmul(side_ps[:, 0:E], ones[:], before[:, KT, :], start=True, stop=True).then_inc(rank_mm, 1)

            def turn_records(k, u):
                pe.wait_ge(rec_t_in[u], 32 * k + 32)
                at_least(pe, xT_done, 4 * k + u)
                for a in range(4):
                    mm = pe.transpose(side_ps[:, a * P:(a + 1) * P], rec_t[u][:, a, 0:F], ident[:])
                mm.then_inc(xT_mm, 1)

            def hidden_units(k, u):
                t, s = 4 * k + u, u % 2
                pe.wait_ge(tile_in[u], 64 * k + 64)
                pe.wait_ge(xT_done, t + 1)
                at_least(pe, hid_done, NH * (t - 1))
                for h in range(NH):
                    mm = pe.matmul(score_ps[:, s, h, :], w1_t[u][:, h * P:(h + 1) * P], xT_t[s], start=True, stop=True)
                mm.then_inc(hid_mm, 1)

            def tile_output(k, u):
                t, s = 4 * k + u, u % 2
                pe.wait_ge(hid_done, NH * (t + 1))
                at_least(pe, y_dve, 4 * (t - 1))
                for a in range(4):
                    for h in range(NH):
                        mm = pe.matmul(ctx_ps[:, s, a * F:(a + 1) * F], hidden[:, s, h, a * P:(a + 1) * P],
                                       w2_t[u][:, h * F:(h + 1) * F], start=(h == 0), stop=(h == NH - 1))
                mm.then_inc(y_mm, 1)

            pe.wait_ge(exp_done, GROUPS * B)
            pe.wait_ge(ctx_out, 16 * B)
            pe.wait_ge(table_dve, 1)

            turn_records(0, 0)
            turn_records(0, 1)
            hidden_units(0, 0)
            for u in (2, 3):
                turn_records(0, u)
                hidden_units(0, u - 1)
                tile_output(0, u - 2)
            with pe.Fori(1, TILES // 4) as k:
                for u in range(4):
                    turn_records(k, u)
                    hidden_units(*back(k, u, 1))
                    tile_output(*back(k, u, 2))
            hidden_units(TILES // 4 - 1, 3)
            tile_output(TILES // 4 - 1, 2)
            tile_output(TILES // 4 - 1, 3)

        @block.scalar
        def _(act):
            def exponentials(i, g):
                G = GROUPS * i + g
                act.wait_ge(qk_done, G + 1)
                at_least(act, clip_done, G - 1)
                act.activation(exps[:, g % 2].rearrange("p h n -> p (h n)"),
                               score_ps[:, g % 2].rearrange("p h n -> p (h n)"), ACT.Exp,
                               scale=SCALE).then_inc(exp_done, 1)

            def copy_context(i, half, kt):
                act.wait_ge(pv_done, GROUPS * i + 16 * half + 2 * kt + 2)
                if kt % 2 == 0:
                    at_least(act, product_done, 8 * (i - 1) + 4 * half + kt // 2 + 1)
                act.activation(ctxu[:, KT * half + kt, :], ctx_ps[:, kt % 2, :], ACT.Copy).then_inc(ctx_out, 1)

            def copy_sums(i, half):
                U = 2 * i + half
                act.wait_ge(pv_done, 16 * (U + 1))
                at_least(act, den_stored, 64 * U)
                act.activation(den[:], den_ps[:], ACT.Copy).then_inc(den_out, 1)

            def store_sums(i, half):
                U = 2 * i + half
                act.wait_ge(den_out, U + 1)
                at_least(act, den_in, 16 * U)
                for h in range(HEADS):
                    row = 64 * (1 - h // 2) + DH * (h % 2)
                    act.dma_start(den_dram[h], den[row:row + KT, :]).then_inc(den_stored, 16)

            def load_sums(i, half):
                U = 2 * i + half
                act.wait_ge(den_stored, 64 * (U + 1))
                at_least(act, rden_done, U)
                act.dma_start(den_sq[:], den_dram.rearrange("h j (a n) -> (h j a) n", n=P)).then_inc(den_in, 16)

            def store_reciprocals(i, half):
                U = 2 * i + half
                act.wait_ge(rden_done, U + 1)
                at_least(act, rdenB_in, 16 * U)
                act.dma_start(rden_dram.rearrange("h j (a n) -> (h j a) n", n=P), rden_sq[:]).then_inc(rden_stored, 16)

            def spread_reciprocals(i, half):
                U = 2 * i + half
                if isinstance(U, int) and U == 0:
                    act.wait_ge(idle_stored, 16 * E)
                act.wait_ge(rden_stored, 16 * (U + 1))
                if half == 1:
                    wait_sum(act, i, 0)
                else:
                    at_least(act, sum_done, 3 * U)
                act.dma_start(rdenB[:].rearrange("p j n -> p (j n)"),
                              rden_dram.rearrange("h j n -> h (j n)").unsqueeze(1).to_broadcast([HEADS, DH, KT * HALF])
                              ).then_inc(rdenB_in, 16)

            def normalise(n, j, src, dst, done, tiles):
                for t in tiles:
                    act.activation(dst[:, t, :], src[:, t, :], ACT.Identity, bias=shift[n][:, t:t + 1],
                                   scale=rstd[n][:, t:t + 1]).then_inc(done, 1)

            def first_norm(j, tiles):
                act.wait_ge(norm_ready[0], 4 * j + 4)
                at_least(act, pre_mm, 8 * (j - 1) + 2)
                at_least(act, xn_stored, 16 * j)
                normalise(0, j, xpre, xn, xn_done, tiles)

            def evacuate(j, u):
                act.wait_ge(pre_mm, 8 * j + u + 1)
                if u < 2:
                    act.activation(xnT[:, u * 512:(u + 1) * 512], side_ps[:], ACT.Copy).then_inc(pre_act, 1)
                else:
                    half, n = u % 2, u // 2 - 2
                    at_least(act, (q_in, k_in)[n][half], 16 * j)
                    if n == 1:
                        at_least(act, k_stored[1 - half], 64 * (j + half))
                    act.activation((q_hi[:, half * HALF:(half + 1) * HALF], k_hi[:])[n], side_ps[:], ACT.Identity,
                                   bias=(bq_c, bk_c)[n][:, 0:1]).then_inc(pre_act, 1)

            def copy_turned(j, half):
                act.wait_ge(g_mm, 3 * j + half + 1)
                act.activation(x3T[:, half * 512:(half + 1) * 512], side_ps[:], ACT.Copy).then_inc(x3T_done, 1)

            act.dma_start(wo[:], WoT).then_inc(consts_in, 16)
            act.dma_start(wg_sb[:], Wg).then_inc(consts_in, 16)
            for t, src in ((bv_b, bv), (bo_b, bo), (gamma_b, gamma), (beta_b, beta), (bg_b, bg), (bias_b, bias)):
                act.dma_start(t[:], src.rearrange("(a f) -> a f", a=1).to_broadcast([P, src.shape[0]])
                              ).then_inc(consts_in, 16)

            act.wait_ge(wproj_in, 16 * 5)
            first_norm(0, range(KT))
            for u in (0, 1, 4, 5, 6, 7):
                evacuate(0, u)
            act.wait_ge(fill_dve, KT + len(BOUNDED) + 1)

            def body(i, att, pre, first, second, third, fourth):
                for g in range(GROUPS):
                    if att:
                        exponentials(i, g)
                        if g % 2 and 5 <= g <= 19:
                            copy_context(i, 0, (g - 5) // 2)
                        if g % 2 and g >= 21:
                            copy_context(i, 1, (g - 21) // 2)
                        if g == 18:
                            copy_sums(i, 0)
                        if g == 19:
                            store_sums(i, 0)
                        if g == 21:
                            load_sums(i, 0)
                        if g == 25:
                            store_reciprocals(i, 0)
                        if g == 28:
                            spread_reciprocals(i, 0)
                    if first:
                        if g in (1, 3):
                            copy_context(i - 1, 1, 6 + g // 2)
                        if g == 2:
                            copy_sums(i - 1, 1)
                        if g == 3:
                            store_sums(i - 1, 1)
                        if g == 7:
                            load_sums(i - 1, 1)
                        if g == 11:
                            store_reciprocals(i - 1, 1)
                        if g == 14:
                            spread_reciprocals(i - 1, 1)
                    if pre:
                        if g in (2, 3, 4, 5):
                            first_norm(i + 1, (2 * g - 4, 2 * g - 3))
                        if g in (6, 8, 14, 17, 23, 29):
                            evacuate(i + 1, {6: 0, 8: 1, 14: 4, 17: 5, 23: 6, 29: 7}[g])
                    if second:
                        if 10 <= g <= 13:
                            act.wait_ge(norm_ready[1], 4 * (i - 2) + 4)
                            normalise(1, i - 2, attn, attn, ln2_done, range(2 * (g - 10), 2 * (g - 9)))
                        if 23 <= g <= 26:
                            act.wait_ge(norm_ready[2], 4 * (i - 2) + 4)
                            at_least(act, g_mm, 3 * (i - 2))
                            at_least(act, x3_stored, 16 * (i - 2))
                            normalise(2, i - 2, x1, x3, x3_done, range(2 * (g - 23), 2 * (g - 22)))
                        if g == 26:
                            at_least(act, g_mm, 3 * (i - 2))
                            copy_turned(i - 2, 0)
                        if g == 31:
                            copy_turned(i - 2, 1)
                    if fourth and g == 6:
                        at_least(act, rec_stored, 32 * KT * (i - 4))
                        act.wait_ge(x3_stored, 16 * (i - 4) + 16)
                        act.dma_start(rec[:, :, 0:F], x3_dram[bass.ds(i - 4, 1)].rearrange("a p (t f) -> p (a t) f", f=F)
                                      ).then_inc(rec_in, 16)
                    if third and g == 17:
                        act.wait_ge(top_dve, STEPS * (i - 3) + 12)
                        act.activation(ed[:], dm[:], ACT.Exp).then_inc(ed_done, 1)

            iterations(act, body)

            def copy_turned_records(k, u):
                t = 4 * k + u
                act.wait_ge(xT_mm, t + 1)
                at_least(act, hid_mm, t - 1)
                act.activation(xT_t[u % 2], side_ps[:], ACT.Copy).then_inc(xT_done, 1)

            def relus(k, u):
                t, s = 4 * k + u, u % 2
                act.wait_ge(hid_mm, t + 1)
                at_least(act, y_mm, t - 1)
                for h in range(NH):
                    act.activation(hidden[:, s, h, :], score_ps[:, s, h, :], ACT.Relu,
                                   bias=b1_t[u][:, h:h + 1]).then_inc(hid_done, 1)

            act.wait_ge(clip_done, GROUPS * B)
            copy_turned_records(0, 0)
            for u in range(1, 4):
                copy_turned_records(0, u)
                relus(0, u - 1)
            with act.Fori(1, TILES // 4) as k:
                for u in range(4):
                    copy_turned_records(k, u)
                    relus(*back(k, u, 1))
            relus(TILES // 4 - 1, 3)

            for j in range(B):
                act.wait_ge(sum_dve, 2 * j + 2)
                act.dma_start(out[j], y_1st[j % 4]).then_inc(out_stored[j % 4], 16)
            for s in range(4):
                act.wait_ge(out_stored[s], 16 * (B // 4))

        @block.vector
        def _(dve):
            def clip(i, g):
                half, kt = g // 16, g % 16 // 2
                G = GROUPS * i + g
                dve.wait_ge(exp_done, G + 1)
                at_least(dve, pv_done, G - 3)
                if kt in ADDED:
                    dve.tensor_scalar(probs[:, g % 4], exps[:, g % 2], E_LO, E_HI, ALU.max, ALU.min
                                      ).then_inc(clip_done, 1)
                else:
                    m = BOUNDED.index(kt)
                    dve.scalar_tensor_tensor(probs[:, g % 4], exps[:, g % 2], E_LO,
                                             clipmask[:, m:m + 1, half * HALF:(half + 1) * HALF].to_broadcast([P, 2, HALF]),
                                             ALU.max, ALU.min).then_inc(clip_done, 1)

            def statistics(n, j, src):
                at_least(dve, norm_ready[n], 4 * j)
                for t in range(KT):
                    ins = dve.bn_stats(st[n][:, t, :], src[:, t, :])
                ins.then_inc(stats[n], 1)
                dve.wait_ge(stats[n], 4 * j + 1)
                s = st[n]
                dve.tensor_tensor(mean2[n][:], s[:, :, 1], s[:, :, 4], ALU.add)
                dve.tensor_tensor(mdif[n][:], s[:, :, 1], s[:, :, 4], ALU.subtract)
                dve.tensor_tensor(vsum[n][:], s[:, :, 2], s[:, :, 5], ALU.add).then_inc(stats[n], 1)
                dve.wait_ge(stats[n], 4 * j + 2)
                dve.scalar_tensor_tensor(mdif2[n][:], mdif[n][:], 0.25, mdif[n][:], ALU.mult, ALU.mult).then_inc(stats[n], 1)
                dve.wait_ge(stats[n], 4 * j + 3)
                dve.scalar_tensor_tensor(var[n][:], vsum[n][:], 1.0 / F, mdif2[n][:], ALU.mult, ALU.add
                                         ).then_inc(stats[n], 1)

            def evacuate(j, u):
                if u < 4:
                    dve.wait_ge(pre_mm, 8 * j + u + 1)
                    at_least(dve, v_in[u - 2], 16 * j)
                    dve.tensor_tensor(vnew[:, 4 * (u - 2):4 * (u - 1), :],
                                      side_ps[:].rearrange("p (t f) -> p t f", t=4),
                                      bv_b[:].unsqueeze(1).to_broadcast([P, 4, F]), ALU.add).then_inc(pre_dve, 1)
                else:
                    half, n = u % 2, u // 2 - 2
                    cols = slice(half * HALF, (half + 1) * HALF)
                    dve.wait_ge(pre_act, 6 * j + u - 1)
                    dve.scalar_tensor_tensor((q_lo[:, cols], k_lo[:])[n], side_ps[:], (bq_c, bk_c)[n][:, 0:1],
                                             (q_hi[:, cols], k_hi[:])[n].bitcast(F32),
                                             ALU.add, ALU.subtract).then_inc(pre_dve, 1)

            def turn_over(j, half):
                U = 2 * j + half
                dve.wait_ge(den_in, 16 * (U + 1))
                at_least(dve, rden_stored, 16 * U)
                dve.reciprocal(rden_sq[:], den_sq[:]).then_inc(rden_done, 1)

            def divide_contexts(j, half, n):
                U = 2 * j + half
                if n == 0:
                    dve.wait_ge(rdenB_in, 16 * (U + 1))
                    dve.wait_ge(ctx_out, 8 * (U + 1))
                kts = slice(2 * n, 2 * n + 2)
                dve.tensor_tensor(rdenB[:, kts, :], ctxu[:, KT * half + 2 * n:KT * half + 2 * n + 2, :],
                                  rdenB[:, kts, :], ALU.mult).then_inc(product_done, 1)

            def sum_last(j, half):
                dve.wait_ge(product_done, 4 * (2 * j + half + 1))
                dve.tensor_tensor(rdenB[:, 0:4, :], rdenB[:, 0:4, :], rdenB[:, 4:8, :], ALU.add).then_inc(last_sum, 1)
                dve.wait_ge(last_sum, 3 * half + 1)
                dve.tensor_tensor(rdenB[:, 0:2, :], rdenB[:, 0:2, :], rdenB[:, 2:4, :], ALU.add).then_inc(last_sum, 1)
                dve.wait_ge(last_sum, 3 * half + 2)
                dve.wait_ge(o_mm, 2 * (j - 1) + half + 1)
                dve.tensor_tensor(ctxn[:, half * HALF:(half + 1) * HALF], rdenB[:, 0, :], rdenB[:, 1, :], ALU.add
                                  ).then_inc(last_sum, 1)

            def residual(j, half):
                dve.wait_ge(o_mm, 2 * j + half + 1)
                dve.wait_ge(xnb_done, j + 1)
                at_least(dve, x1_done, 2 * j)
                dve.tensor_tensor(attn[:, 4 * half:4 * half + 4, :], side_ps[:].rearrange("p (t f) -> p t f", t=4),
                                  xnpost[:, 4 * half:4 * half + 4, :], ALU.add).then_inc(o_done, 1)

            def top_step(j, n):
                lanes = lambda v: v[:].unsqueeze(2).to_broadcast([P, KT, E])
                ranks = rank[:].unsqueeze(1).to_broadcast([P, KT, E])
                if n > 1:
                    dve.wait_ge(top_dve, STEPS * j + n - 1)
                if n == 1:
                    dve.wait_ge(g_mm, 3 * j + 3)
                    ins = dve.tensor_tensor(lg[:], side_ps[:, 0:KT * E].rearrange("p (t e) -> p t e", e=E),
                                            gateb[:].unsqueeze(1).to_broadcast([P, KT, E]), ALU.add)
                elif n == 2:
                    ins = dve.tensor_reduce(m1[:], lg[:], AX_X, ALU.max)
                elif n == 3:
                    ins = dve.tensor_tensor(eq[:], lg[:], lanes(m1), ALU.is_equal)
                elif n == 4:
                    ins = dve.tensor_tensor(cand[:], eq[:], ranks, ALU.mult)
                elif n == 5:
                    ins = dve.tensor_reduce(r1[:], cand[:], AX_X, ALU.max)
                elif n == 6:
                    ins = dve.tensor_tensor(oh1[:], ranks, lanes(r1), ALU.is_equal)
                elif n == 7:
                    ins = dve.scalar_tensor_tensor(lg2[:], oh1[:], -FAR, lg[:], ALU.mult, ALU.add)
                elif n == 8:
                    ins = dve.tensor_reduce(m2[:], lg2[:], AX_X, ALU.max)
                elif n == 9:
                    ins = dve.tensor_tensor(eq[:], lg2[:], lanes(m2), ALU.is_equal)
                elif n == 10:
                    ins = dve.tensor_tensor(cand[:], eq[:], ranks, ALU.mult)
                elif n == 11:
                    ins = dve.tensor_reduce(r2[:], cand[:], AX_X, ALU.max)
                elif n == 12:
                    ins = dve.tensor_tensor(dm[:], m2[:], m1[:], ALU.subtract)
                elif n == 13:
                    ins = dve.tensor_tensor(oh2[:], ranks, lanes(r2), ALU.is_equal)
                elif n == 14:
                    dve.wait_ge(ed_done, j + 1)
                    ins = dve.tensor_scalar(es[:], ed[:], 1.0, None, ALU.add)
                elif n == 15:
                    ins = dve.reciprocal(w1st[:], es[:])
                elif n == 16:
                    ins = dve.tensor_tensor(w2nd[:], ed[:], w1st[:], ALU.mult)
                elif n == 17:
                    ins = dve.tensor_tensor(cmb1[:], oh1[:], lanes(w1st), ALU.mult)
                elif n == 18:
                    ins = dve.tensor_tensor(cmb2[:], oh2[:], lanes(w2nd), ALU.mult)
                else:
                    ins = dve.tensor_tensor(comb[:], cmb1[:], cmb2[:], ALU.add)
                ins.then_inc(top_dve, 1)

            dve.wait_ge(xpre_in, 16)

            def count_tokens(j):
                dve.wait_ge(top_dve, STEPS * j + 13)
                at_least(dve, rank_mm, j)
                at_least(dve, count_dve, RANKS * j)
                dve.tensor_tensor(chosen[:], oh1[:], oh2[:], ALU.add).then_inc(count_dve, 1)
                dve.tensor_copy(before[:, 0, :], before[:, KT, :]).then_inc(count_dve, 1)
                for t in range(KT):
                    dve.wait_ge(count_dve, RANKS * j + 2 + t)
                    dve.tensor_tensor(before[:, t + 1, :], before[:, t, :], chosen[:, t, :], ALU.add).then_inc(count_dve, 1)

            def slots_of(j):
                dve.wait_ge(rank_mm, j + 1)
                at_least(dve, slot_dve, 6 * j)
                dve.tensor_tensor(slot[:], side_ps[:, KT * E:2 * KT * E].rearrange("p (t e) -> p t e", e=E),
                                  region0[:].unsqueeze(1).to_broadcast([P, KT, E]), ALU.add).then_inc(slot_dve, 1)

            def place_records(j):
                dve.wait_ge(top_dve, STEPS * j + STEPS)
                dve.wait_ge(slot_dve, 6 * j + 1)
                at_least(dve, rec_stored, 32 * KT * j)
                dve.tensor_copy(rec[:, :, F:F + E], comb[:])
                dve.scalar_tensor_tensor(rec[:, :, F + E:REC], oh2[:], float(T),
                                         token[:].unsqueeze(2).to_broadcast([P, KT, E]), ALU.mult, ALU.add)
                dve.tensor_tensor(in1[:], slot[:], oh1[:], ALU.mult).then_inc(slot_dve, 1)
                dve.tensor_tensor(in2[:], slot[:], oh2[:], ALU.mult).then_inc(slot_dve, 1)
                dve.wait_ge(slot_dve, 6 * j + 3)
                dve.tensor_scalar(token[:], token[:], float(N), None, ALU.add)
                dve.tensor_reduce(slot_f[:, 0, :], in1[:], AX_X, ALU.add).then_inc(slot_dve, 1)
                dve.tensor_reduce(slot_f[:, 1, :], in2[:], AX_X, ALU.add).then_inc(slot_dve, 1)
                dve.wait_ge(slot_dve, 6 * j + 5)
                dve.tensor_copy(slot_i[:], slot_f[:]).then_inc(slot_dve, 1)


            dve.wait_ge(xpre_in, 16)
            statistics(0, 0, xpre)
            dve.wait_ge(wproj_in, 16 * 5)
            dve.wait_ge(consts_in, 16 * 8)
            for u in range(2, 7):
                evacuate(0, u)
            for t in range(KT):
                dve.wait_ge(adj_in, 16 * KT)
                if t in ADDED:
                    dve.tensor_scalar(addmask[:, ADDED.index(t), :], adj_sb[:, t, :].bitcast(I32), 0.0, NO_EDGE,
                                      ALU.is_equal, ALU.mult).then_inc(fill_dve, 1)
                else:
                    dve.tensor_scalar(clipmask[:, BOUNDED.index(t), :], adj_sb[:, t, :].bitcast(I32), 0.0, E_HI,
                                      ALU.not_equal, ALU.mult).then_inc(fill_dve, 1)
            dve.wait_ge(fill_dve, KT)
            for m in range(len(BOUNDED)):
                dve.tensor_scalar(clipmask[:, m, :], clipmask[:, m, :], E_LO, None, ALU.max).then_inc(fill_dve, 1)
            dve.tensor_tensor(gateb[:], bg_b[:], bias_b[:], ALU.add).then_inc(fill_dve, 1)
            evacuate(0, 7)
            dve.wait_ge(fill_dve, KT + len(BOUNDED) + 1)
            dve.wait_ge(xpre_in, 32)
            statistics(0, 1, xpre)

            def body(i, att, pre, first, second, third, fourth):
                for g in range(GROUPS):
                    if att:
                        clip(i, g)
                        if g == 23:
                            turn_over(i, 0)
                    if first:
                        if g in (1, 3, 5, 7):
                            divide_contexts(i - 1, 0, g // 2)
                        if g == 9:
                            turn_over(i - 1, 1)
                        if g == 20:
                            residual(i - 1, 0)
                        if g in (17, 19, 21, 23):
                            divide_contexts(i - 1, 1, g // 2 - 8)
                    if first and isinstance(i, int) and i == B and g in (8, 23):
                        sum_last(i - 1, g // 16)
                    if fourth and g == 1:
                        slots_of(i - 4)
                    if fourth and g == 5:
                        place_records(i - 4)
                    if third:
                        if 1 <= g <= 13:
                            top_step(i - 3, g)
                        if g == 16:
                            count_tokens(i - 3)
                        if 18 <= g <= 23:
                            top_step(i - 3, g - 4)
                    if second:
                        if g == 3:
                            residual(i - 2, 1)
                        if g == 4:
                            dve.wait_ge(o_done, 2 * (i - 2) + 2)
                            statistics(1, i - 2, attn)
                        if g == 21:
                            dve.wait_ge(x1_done, 2 * (i - 2) + 2)
                            statistics(2, i - 2, x1)
                    if pre:
                        if g == 26 and (not isinstance(i, int) or i + 2 < B):
                            dve.wait_ge(xpre_in, 16 * (i + 2) + 16)
                            statistics(0, i + 2, xpre)
                        if g in (9, 11, 15, 17, 23, 28):
                            evacuate(i + 1, {9: 2, 11: 3, 15: 4, 17: 5, 23: 6, 28: 7}[g])

            iterations(dve, body, last=B - 3)

            at = lambda v, n: v.unsqueeze(1).to_broadcast([P, n, E])
            dve.wait_ge(rank_mm, B + 1)
            dve.wait_ge(tail_made, 5)
            dve.wait_ge(product_done, 8 * B)
            dve.tensor_copy(total, side_ps[:, 0:E]).then_inc(table_dve, 1)
            dve.wait_ge(table_dve, 1)
            dve.tensor_tensor(tail_f, total, region0[:], ALU.add)
            dve.tensor_tensor(more, total.unsqueeze(2).to_broadcast([P, E, T // TILE]),
                              bounds.unsqueeze(1).to_broadcast([P, E, T // TILE]), ALU.is_gt).then_inc(table_dve, 1)
            dve.wait_ge(table_dve, 2)
            dve.tensor_copy(tail_i, tail_f)
            dve.tensor_reduce(tiles_of, more, AX_X, ALU.add).then_inc(table_dve, 1)
            dve.wait_ge(table_dve, 3)
            dve.tensor_scalar(step_of, tiles_of, -float(TILE), float(REGION), ALU.mult, ALU.add)
            dve.tensor_copy(upto[:, 0:1], tiles_of[:, 0:1]).then_inc(table_dve, 1)
            for e in range(1, E):
                dve.wait_ge(table_dve, 3 + e)
                dve.tensor_tensor(upto[:, e:e + 1], upto[:, e - 1:e], tiles_of[:, e:e + 1], ALU.add).then_inc(table_dve, 1)
            dve.wait_ge(table_dve, 3 + E)
            dve.tensor_tensor(reached, index_t.unsqueeze(2).to_broadcast([P, TILES, E]), at(upto, TILES), ALU.is_ge)
            dve.tensor_scalar(beyond, index_t, upto[:, E - 1:E], None, ALU.subtract).then_inc(table_dve, 1)
            dve.wait_ge(table_dve, 4 + E)
            dve.tensor_tensor(weighed, reached, at(step_of, TILES), ALU.mult)
            dve.tensor_reduce(expert_f, reached, AX_X, ALU.add)
            dve.tensor_scalar(pick[:, :, 0], reached[:, :, 0], -1.0, 1.0, ALU.mult, ALU.add)
            dve.tensor_tensor(pick[:, :, 1:E], reached[:, :, 0:E - 1], reached[:, :, 1:E], ALU.subtract
                              ).then_inc(table_dve, 1)
            dve.wait_ge(table_dve, 5 + E)
            dve.tensor_reduce(start_f, weighed, AX_X, ALU.add)
            dve.tensor_scalar(expert_f, expert_f, float(E - 1), None, ALU.min).then_inc(table_dve, 1)
            dve.wait_ge(table_dve, 6 + E)
            dve.tensor_tensor(weighed, beyond.unsqueeze(2).to_broadcast([P, TILES, E]), at(index_e, TILES),
                              ALU.is_equal).then_inc(table_dve, 1)
            dve.scalar_tensor_tensor(start_f, index_t, float(TILE), start_f, ALU.mult, ALU.add)
            dve.tensor_copy(expert_i, expert_f).then_inc(table_dve, 1)
            dve.wait_ge(table_dve, 8 + E)
            dve.tensor_copy(start_i, start_f).then_inc(table_dve, 1)
            dve.tensor_tensor(pick, pick, weighed, ALU.add).then_inc(table_dve, 1)
            dve.wait_ge(table_dve, TABLE)

            def finish_tile(k, u):
                t, s = 4 * k + u, u % 2
                dve.wait_ge(picked_done, t + 1)
                dve.tensor_reduce(wd_t[s], picked[s].rearrange("p a (c e) -> p a c e", e=E), AX_X, ALU.add
                                  ).then_inc(y_dve, 1)
                at_least(dve, y_stored[u], 64 * k)
                dve.wait_ge(y_mm, t + 1)
                dve.tensor_tensor(y_t[u], ctx_ps[:, s, :].rearrange("p (a f) -> p a f", a=4),
                                  b2_t[u].unsqueeze(1).to_broadcast([P, 4, F]), ALU.add).then_inc(y_dve, 1)
                dve.wait_ge(y_dve, 4 * t + 2)
                dve.tensor_copy(row_t[u], wd_t[s][:, :, 1]).then_inc(y_dve, 1)
                for a in range(4):
                    ins = dve.tensor_scalar(y_t[u][:, a, :], y_t[u][:, a, :], wd_t[s][:, a, 0:1], None, ALU.mult)
                ins.then_inc(y_dve, 1)

            for u in range(4):
                finish_tile(0, u)
            with dve.Fori(1, TILES // 4) as k:
                for u in range(4):
                    finish_tile(k, u)

            dve.wait_ge(x1_in, 16 * B)
            for j in range(B):
                dve.wait_ge(sum_in[j % 4], 32 * (j // 4) + 32)
                dve.tensor_tensor(y_1st[j % 4], x1_all[j], y_1st[j % 4], ALU.add).then_inc(sum_dve, 1)
                dve.wait_ge(sum_dve, 2 * j + 1)
                dve.tensor_tensor(y_1st[j % 4], y_1st[j % 4], y_2nd[j % 4], ALU.add).then_inc(sum_dve, 1)

        @block.gpsimd
        def _(pool):
            pool.memset(ident[:], 0.0).then_inc(fills, 1)
            pool.memset(onehot[:], 0.0).then_inc(fills, 1)
            pool.memset(eps8[:], EPS).then_inc(fills, 1)
            pool.memset(mhalf8[:], -0.5).then_inc(fills, 1)
            pool.iota(rank[:], pattern=[[-1, E]], base=E, channel_multiplier=0,
                      allow_small_or_imprecise_dtypes=True).then_inc(fills, 1)
            pool.memset(ones[:], 1.0).then_inc(fills, 1)
            pool.memset(before[:, KT, :], 0.0).then_inc(fills, 1)
            pool.iota(region0[:], pattern=[[REGION, E]], base=0, channel_multiplier=0,
                      allow_small_or_imprecise_dtypes=True).then_inc(fills, 1)
            pool.iota(token[:], pattern=[[P, KT]], base=0, channel_multiplier=1,
                      allow_small_or_imprecise_dtypes=True).then_inc(fills, 1)
            pool.wait_ge(fills, 9)
            pool.affine_select(out=tri[:], in_=ones[:], compare_op=ALU.is_gt, fill=0.0, base=0,
                               pattern=[[1, P]], channel_multiplier=-1).then_inc(fills, 1)
            pool.affine_select(out=ident[:], in_=ident[:], compare_op=ALU.not_equal, fill=1.0, base=0,
                               pattern=[[-1, P]], channel_multiplier=1).then_inc(fills, 1)
            for t in range(KT):
                pool.memset(onehot[:, t, t:t + 1], 1.0).then_inc(fills, 1)
            pool.wait_ge(fills, 11 + KT)
            pool.tensor_copy(ident16[:], ident[:]).then_inc(fills, 1)

            def fill(records, area, made):
                pool.memset(records, 0.0).then_inc(made, 1)
                pool.wait_ge(made, 1)
                pool.iota(records[:, :, F + E:REC], pattern=[[P, 4], [TILE, E]], base=2 * T + area * TILE,
                          channel_multiplier=1, allow_small_or_imprecise_dtypes=True).then_inc(made, 1)

            fill(idle_fill, E, idle_made)

            def scale_and_shift(n, j, used):
                pool.wait_ge(stats[n], 4 * j + 4)
                at_least(pool, used, KT * j)
                pool.tensor_tensor(veps[n][:], var[n][:], eps8[:], ALU.add).then_inc(norm_ready[n], 1)
                pool.wait_ge(norm_ready[n], 4 * j + 1)
                pool.tensor_tensor(rstd[n][:], veps[n][:], mhalf8[:], ALU.pow).then_inc(norm_ready[n], 1)
                pool.wait_ge(norm_ready[n], 4 * j + 2)
                pool.tensor_tensor(nm[n][:], mean2[n][:], rstd[n][:], ALU.mult).then_inc(norm_ready[n], 1)
                pool.wait_ge(norm_ready[n], 4 * j + 3)
                pool.tensor_tensor(shift[n][:], nm[n][:], mhalf8[:], ALU.mult).then_inc(norm_ready[n], 1)

            pool.wait_ge(fills, FILLS)
            scale_and_shift(0, 0, xn_done)
            scale_and_shift(0, 1, xn_done)
            pool.wait_ge(consts_in, 16 * 8)

            def sum_key_tiles(j, half):
                U = 2 * j + half
                pool.wait_ge(product_done, 4 * (U + 1))
                pool.tensor_tensor(rdenB[:, 0:4, :], rdenB[:, 0:4, :], rdenB[:, 4:8, :], ALU.add).then_inc(sum_done, 1)
                pool.wait_ge(sum_done, 3 * U + 1)
                pool.tensor_tensor(rdenB[:, 0:2, :], rdenB[:, 0:2, :], rdenB[:, 2:4, :], ALU.add).then_inc(sum_done, 1)
                pool.wait_ge(sum_done, 3 * U + 2)
                at_least(pool, o_mm, 2 * (j - 1) + half + 1)
                pool.tensor_tensor(ctxn[:, half * HALF:(half + 1) * HALF], rdenB[:, 0, :], rdenB[:, 1, :], ALU.add
                                   ).then_inc(sum_done, 1)

            def scatter_records(j, tiles):
                for t in tiles:
                    for n in range(2):
                        pool.indirect_dma_start(rec_dram, bass.IndirectOffsetOnAxis(ap=slot_i[:, n, t:t + 1], axis=0),
                                                rec[:, t, :], None
                                                ).then_inc(rec_stored, 16)

            def prepare_table():
                pool.wait_ge(product_done, 8 * B)
                pool.wait_ge(last_sum, 6)
                fill(tail_fill, 0, tail_made)
                for v, step in ((index_t, 1), (index_e, 1), (bounds, TILE)):
                    pool.iota(v, pattern=[[step, v.shape[1]]], base=0, channel_multiplier=0,
                              allow_small_or_imprecise_dtypes=True).then_inc(tail_made, 1)

            def body(i, att, pre, first, second, third, fourth):
                wide = lambda v: v[:].unsqueeze(1).to_broadcast([P, KT, F])
                if isinstance(i, int) and i == B + 3:
                    prepare_table()
                if second:
                    scale_and_shift(1, i - 2, ln2_done)
                if first and not (isinstance(i, int) and i == B):
                    sum_key_tiles(i - 1, 0)
                if fourth:
                    pool.wait_ge(fills, FILLS)
                    pool.wait_ge(slot_dve, 6 * (i - 4) + 6)
                    pool.wait_ge(rec_in, 16 * (i - 4) + 16)
                    scatter_records(i - 4, (0, 1))
                if first:
                    pool.wait_ge(post_in, 16 * (i - 1) + 16)
                    pool.tensor_tensor(xnpost[:], xnpost[:], wide(bo_b), ALU.add).then_inc(xnb_done, 1)
                if second:
                    pool.wait_ge(ln2_done, KT * (i - 2) + KT)
                    pool.tensor_tensor(attn[:], attn[:], wide(gamma_b), ALU.mult).then_inc(x1_done, 1)
                    pool.wait_ge(x1_done, 2 * (i - 2) + 1)
                    pool.wait_ge(xpb_done, (i - 2) + 1)
                    at_least(pool, x3_done, KT * (i - 2))
                    at_least(pool, x1_stored, 16 * (i - 2))
                    pool.tensor_tensor(x1[:], attn[:], xpost[:], ALU.add).then_inc(x1_done, 1)
                if fourth:
                    scatter_records(i - 4, (2, 3))
                if second:
                    scale_and_shift(2, i - 2, x3_done)
                if first:
                    pool.wait_ge(xpost_in, 16 * (i - 1) + 16)
                    pool.tensor_tensor(xpost[:], xpost[:], wide(beta_b), ALU.add).then_inc(xpb_done, 1)
                    if not (isinstance(i, int) and i == B):
                        sum_key_tiles(i - 1, 1)
                if fourth:
                    scatter_records(i - 4, (4, 5, 6, 7))
                if pre and (not isinstance(i, int) or i + 2 < B):
                    scale_and_shift(0, i + 2, xn_done)

            iterations(pool, body, last=B - 3)

            def pick_weights(k, u):
                pool.wait_ge(rec_t_in[u], 32 * k + 32)
                pool.tensor_tensor(picked[u % 2], rec_t[u][:, :, F:REC],
                                   pick2_t[u].unsqueeze(1).to_broadcast([P, 4, 2 * E]), ALU.mult).then_inc(picked_done, 1)

            def scatter_outputs(k, last):
                for u in range(4):
                    pool.wait_ge(y_dve, 4 * (4 * k + u) + 4)
                    if u < 3:
                        pick_weights(k, u + 1)
                    elif not last:
                        pick_weights(k + 1, 0)
                    for a in range(4):
                        pool.indirect_dma_start(y_dram, bass.IndirectOffsetOnAxis(ap=row_t[u][:, a:a + 1], axis=0),
                                                y_t[u][:, a, :], None).then_inc(y_stored[u], 16)

            pick_weights(0, 0)
            with pool.Fori(0, TILES // 4 - 1) as k:
                scatter_outputs(k, False)
            scatter_outputs(TILES // 4 - 1, True)



_INS = ["x", "adjT", "WqT", "WkT", "WvT", "WoT", "bq", "bk", "bv", "bo", "gamma", "beta",
        "Wg", "bg", "bias", "W1", "b1", "W2", "b2"]


def kernel(x, adj, L0_gnn_Wq, L0_gnn_bq, L0_gnn_Wk, L0_gnn_bk, L0_gnn_Wv, L0_gnn_bv, L0_gnn_Wo, L0_gnn_bo,
           L0_gnn_gamma, L0_gnn_beta, L0_ffn_Wg, L0_ffn_bg, L0_ffn_bias, L0_ffn_W1, L0_ffn_b1, L0_ffn_W2, L0_ffn_b2):
    import concourse.bacc as bacc
    from concourse.bass_utils import run_bass_kernel_spmd

    B, N, F = x.shape
    E, _, HID = L0_ffn_W1.shape
    KT, NH = N // P, HID // P
    flat = lambda a: np.ascontiguousarray(np.asarray(a))
    laid = {
        "x": flat(np.asarray(x).reshape(B, KT, P, F).transpose(0, 2, 1, 3).reshape(B, P, KT * F)),
        "adjT": flat(np.asarray(adj).T),
        "WqT": flat(np.asarray(L0_gnn_Wq).T), "WkT": flat(np.asarray(L0_gnn_Wk).T),
        "WvT": flat(np.asarray(L0_gnn_Wv).T), "WoT": flat(np.asarray(L0_gnn_Wo).T),
        "bq": flat(L0_gnn_bq), "bk": flat(L0_gnn_bk), "bv": flat(L0_gnn_bv), "bo": flat(L0_gnn_bo),
        "gamma": flat(L0_gnn_gamma), "beta": flat(L0_gnn_beta),
        "Wg": flat(L0_ffn_Wg), "bg": flat(L0_ffn_bg), "bias": flat(L0_ffn_bias),
        "W1": flat(L0_ffn_W1),
        "b1": flat(np.asarray(L0_ffn_b1).reshape(E, NH, P).transpose(0, 2, 1)),
        "W2": flat(np.asarray(L0_ffn_W2).reshape(E, NH, P, F).transpose(0, 2, 1, 3).reshape(E, P, NH * F)),
        "b2": flat(L0_ffn_b2),
    }
    nc = bacc.Bacc("TRN2", target_bir_lowering=False, num_devices=1)
    args = [nc.dram_tensor(f"in_{n}", laid[n].shape, mybir.dt.from_np(laid[n].dtype), kind="ExternalInput").ap()
            for n in _INS]
    out = nc.dram_tensor("out_0", (B, P, KT * F), F32, kind="ExternalOutput").ap()
    gnn_moe_kernel(nc, *args, out)
    got = run_bass_kernel_spmd(nc, [{f"in_{n}": laid[n] for n in _INS}], core_ids=[0]).results[0]["out_0"]
    return np.ascontiguousarray(got.reshape(B, P, KT, F).transpose(0, 2, 1, 3).reshape(B, N, F))
```
